# Optimizing a Trainium2 kernel written in Bass

```python
import numpy as np
import jax
import jax.numpy as jnp

def _softmax(x, axis=-1):
    return jax.nn.softmax(x, axis=axis)
def _gelu(x):
    return jax.nn.gelu(x, approximate=True)
def _silu(x):
    return jax.nn.silu(x)
def _sigmoid(x):
    return jax.nn.sigmoid(x)
def _layernorm(x, axis=-1, eps=1e-5):
    m = jnp.mean(x, axis=axis, keepdims=True)
    v = jnp.var(x, axis=axis, keepdims=True)
    return (x - m) / jnp.sqrt(v + eps)
def _scatter_add(tgt, idx, src, axis=0):
    return tgt.at[idx].add(src)
def _segment_sum(src, seg, n):
    return jax.ops.segment_sum(src, seg, n)

kernel_name = 'mk_conv_seq_d1_conv_nchw256_38e6be'

def setup_inputs(seed: int = 0):
    np.random.seed(seed)
    _w = jnp.asarray
    def _rec_inputs():
        import jax
        import jax.numpy as jnp
        _gk = jax.random.key(seed)
        x = -0.0003929 + 0.9999 * jax.random.normal(jax.random.fold_in(_gk, 1), (16, 256, 64, 64), jnp.float32)
        return x
    x = _rec_inputs()
    def _L0_conv_setup():
        import jax, jax.numpy as jnp
        import numpy as np
        B, C, H, W = (16, 256, 64, 64)
        DIM = 8
        HEADS = C // DIM
        TD = HEADS * DIM
        EPS = 1e-15
        BN_EPS = 1e-05
        key = jax.random.key(seed)
        ks = jax.random.split(key, 7)
        s = 0.05
        return {'x': jax.random.normal(ks[0], (B, C, H, W), jnp.float32), 'w_qkv': jax.random.normal(ks[1], (3 * TD, C), jnp.float32) * s, 'w_dw': jax.random.normal(ks[2], (3 * TD, 1, 5, 5), jnp.float32) * s, 'w_pw': jax.random.normal(ks[3], (3 * TD, DIM), jnp.float32) * s, 'w_proj': jax.random.normal(ks[4], (C, 2 * TD), jnp.float32) * s, 'bn_gamma': jnp.ones((C,), jnp.float32), 'bn_beta': jnp.zeros((C,), jnp.float32), 'bn_mean': jax.random.normal(ks[5], (C,), jnp.float32) * 0.1, 'bn_var': jax.random.uniform(ks[6], (C,), jnp.float32, 0.5, 1.5)}
    _L0_conv_all = _L0_conv_setup()
    _L0_conv_in = {k: v for k, v in _L0_conv_all.items() if k in ('w_qkv', 'w_dw', 'w_pw', 'w_proj', 'bn_gamma', 'bn_beta', 'bn_mean', 'bn_var', )}
    del _L0_conv_all

    return {
        "x": x,
        "L0_conv_w_qkv": _L0_conv_in["w_qkv"],
        "L0_conv_w_dw": _L0_conv_in["w_dw"],
        "L0_conv_w_pw": _L0_conv_in["w_pw"],
        "L0_conv_w_proj": _L0_conv_in["w_proj"],
        "L0_conv_bn_gamma": _L0_conv_in["bn_gamma"],
        "L0_conv_bn_beta": _L0_conv_in["bn_beta"],
        "L0_conv_bn_mean": _L0_conv_in["bn_mean"],
        "L0_conv_bn_var": _L0_conv_in["bn_var"],
    }

def reference(x, L0_conv_w_qkv, L0_conv_w_dw, L0_conv_w_pw, L0_conv_w_proj, L0_conv_bn_gamma, L0_conv_bn_beta, L0_conv_bn_mean, L0_conv_bn_var):
    import jax
    import jax.numpy as jnp
    def _L0_conv_ref(x, w_qkv, w_dw, w_pw, w_proj, bn_gamma, bn_beta, bn_mean, bn_var):
        import jax, jax.numpy as jnp
        import numpy as np
        B, C, H, W = (16, 256, 64, 64)
        DIM = 8
        HEADS = C // DIM
        TD = HEADS * DIM
        EPS = 1e-15
        BN_EPS = 1e-05
        qkv = jnp.einsum('bchw,oc->bohw', x, w_qkv)
        dw = jax.lax.conv_general_dilated(qkv, w_dw, window_strides=(1, 1), padding=[(2, 2), (2, 2)], dimension_numbers=('NCHW', 'OIHW', 'NCHW'), feature_group_count=3 * TD)
        G = 3 * HEADS
        dwg = dw.reshape(B, G, DIM, H, W)
        wg = w_pw.reshape(G, DIM, DIM)
        agg = jnp.einsum('bgihw,goi->bgohw', dwg, wg).reshape(B, 3 * TD, H, W)
        qkv_ms = jnp.concatenate([qkv, agg], axis=1)
        h2 = qkv_ms.shape[1] // (3 * DIM)
        t = qkv_ms.reshape(B, h2, 3 * DIM, H * W)
        q = jax.nn.relu(t[:, :, :DIM])
        k = jax.nn.relu(t[:, :, DIM:2 * DIM])
        v = t[:, :, 2 * DIM:]
        v = jnp.concatenate([v, jnp.ones_like(v[:, :, :1])], axis=2)
        vk = jnp.einsum('bhen,bhdn->bhed', v, k)
        out = jnp.einsum('bhed,bhdn->bhen', vk, q)
        out = out[:, :, :-1] / (out[:, :, -1:] + EPS)
        out = out.reshape(B, h2 * DIM, H, W)
        y = jnp.einsum('bchw,oc->bohw', out, w_proj)
        scale = (bn_gamma / jnp.sqrt(bn_var + BN_EPS))[None, :, None, None]
        y = (y - bn_mean[None, :, None, None]) * scale + bn_beta[None, :, None, None]
        return x + y

    def _gn(v, G=32, eps=1e-5):
        B_, C_, H_, W_ = v.shape
        g = v.reshape(B_, G, C_ // G, H_, W_)
        m = jnp.mean(g, axis=(2, 3, 4), keepdims=True)
        s = jnp.var(g, axis=(2, 3, 4), keepdims=True)
        return ((g - m) / jnp.sqrt(s + eps)).reshape(v.shape)

    def _ln_c(v, eps=1e-6):
        m = jnp.mean(v, axis=1, keepdims=True)
        s = jnp.var(v, axis=1, keepdims=True)
        return (v - m) / jnp.sqrt(s + eps)

    def _ln_t(v, eps=1e-5):
        m = jnp.mean(v, axis=-1, keepdims=True)
        s = jnp.var(v, axis=-1, keepdims=True)
        return (v - m) / jnp.sqrt(s + eps)

    def _to_tokens(v):
        B_, C_, H_, W_ = v.shape
        return v.reshape(B_, C_, H_ * W_).transpose(0, 2, 1)
    def _from_tokens(t, like):
        B_, C_, H_, W_ = like.shape
        return t.transpose(0, 2, 1).reshape(B_, C_, H_, W_)

    x = _L0_conv_ref(x, L0_conv_w_qkv, L0_conv_w_dw, L0_conv_w_pw, L0_conv_w_proj, L0_conv_bn_gamma, L0_conv_bn_beta, L0_conv_bn_mean, L0_conv_bn_var)
    return x


_drawn_inputs = setup_inputs


def setup_inputs(seed=0):
    import zlib

    import numpy as np

    out = dict(_drawn_inputs(seed))
    spreads = {'L0_conv_bn_gamma': (1.0, 0.6), 'L0_conv_bn_beta': (0.0, 0.1)}
    factors = {'L0_conv_w_dw': 8.0, 'L0_conv_w_pw': 8.0, 'L0_conv_bn_var': 3.41}
    for name, (base, spread) in spreads.items():
        noise = np.random.default_rng([zlib.crc32(name.encode()), seed]).standard_normal(out[name].shape)
        drawn = base * np.exp(spread * noise) if base else spread * noise
        out[name] = jnp.asarray(drawn.astype(out[name].dtype))
    for name, factor in factors.items():
        out[name] = (out[name] * factor).astype(out[name].dtype)
    return out
```

```python
from contextlib import ExitStack

import concourse.bass as bass
from concourse import mybir

F32 = mybir.dt.float32
F32R = mybir.dt.float32r
ALU = mybir.AluOpType
ACT = mybir.ActivationFunctionType
AX_X = mybir.AxisListType.X

P = 128
C = 256
H = W = 64
NPIX = H * W
DIM = 8
HEADS = C // DIM
KT = C // P
PATCH = 4
NPL = PATCH * PATCH
NB = H // PATCH
PLANE = NB * NB
GS = NB + 1
GRID = GS * GS
STG = NPL * GRID
TAPS = 5
PADK = 11
KROW = DIM * PADK * PADK
RWIN = KROW - 3 * PADK - 3
BANK = 512
HT = P // DIM
PARTS = 3
EPS = 1e-15
BN_EPS = 1e-5


class Mem:

    def __init__(self, nc, ctx):
        self.nc, self.ctx = nc, ctx

    def sb(self, name, shape, dt=F32):
        return self.ctx.enter_context(self.nc.sbuf_tensor(name, shape, dt))

    def ps(self, name, shape=(P, BANK)):
        return self.ctx.enter_context(self.nc.psum_tensor(name, list(shape), F32))

    def sem(self, name):
        return self.ctx.enter_context(self.nc.semaphore(name))


def split_passes(hi_w, lo_w, hi_x, lo_x):
    return ((hi_w, hi_x), (lo_w, hi_x), (hi_w, lo_x))


def phase0_weights(nc, keep, w_qkv, w_dw, w_pw, w_proj, bn_gamma, bn_beta, bn_mean, bn_var, kern_d):
    G = PARTS * HEADS
    with ExitStack() as ctx:
        m = Mem(nc, ctx)
        wq_nat = m.sb("wq_nat", [P, PARTS * KT, C])
        wp_nat = m.sb("wp_nat", [P, KT, 2 * C])
        dw_sb = m.sb("dw_sb", [G, DIM, TAPS * TAPS])
        pw_sb = m.sb("pw_sb", [G, DIM, DIM])
        kern = m.sb("kern_sb", [G, DIM, DIM, PADK, PADK])
        bn_sb = m.sb("bn_sb", [P, 4, KT])
        bn_t = m.sb("bn_t", [P, 2, KT])
        bn_r = m.sb("bn_r", [P, KT])
        ps = [m.ps(f"ps0_{i}") for i in range(4)]
        s_w = m.sem("p0_w_loaded")
        s_c = m.sem("p0_conv_loaded")
        s_b = m.sem("p0_bn_loaded")
        s_mask = m.sem("p0_masks")
        s_tp = m.sem("p0_transposed")
        s_hi = m.sem("p0_hi_made")
        s_lo = m.sem("p0_lo_made")
        s_v = m.sem("p0_vector_step")
        s_bn = m.sem("p0_bn_root")
        s_kern = m.sem("p0_kernels_made")
        s_st = m.sem("p0_kernels_stored")
        jobs = [("q", o, kt) for kt in range(KT) for o in range(PARTS * KT)] \
            + [("p", t, ot) for ot in range(KT) for t in range(2 * KT)]

        def source(job):
            kind, a, b = job
            return wq_nat[:, a, b * P:(b + 1) * P] if kind == "q" else wp_nat[:, b, a * P:(a + 1) * P]

        def target(job, which):
            kind, a, b = job
            if kind == "q":
                return keep[f"wq_{which}"][:, b, a * P:(a + 1) * P]
            return keep[f"wp_{which}"][:, a, b * P:(b + 1) * P]

        with nc.Block() as block:
            @block.sync
            def _(sp):
                w_v = w_qkv.rearrange("(h j i) c -> j h i c", j=PARTS, i=DIM)
                for j in range(PARTS):
                    for half in range(KT):
                        sp.dma_start(wq_nat[:, j * KT + half, :],
                                     w_v[j, half * HT:(half + 1) * HT]).then_inc(s_w, 16)
                sp.dma_start(wp_nat[:], w_proj.rearrange("(t p) c -> p t c", p=P)).then_inc(s_w, 16)
                sp.wait_ge(s_kern, 1)
                sp.dma_start(kern_d.rearrange("g i k -> g (i k)"),
                             kern[:].rearrange("g i o a b -> g (i o a b)")).then_inc(s_st, 16)
                sp.wait_ge(s_st, 16)

            @block.scalar
            def _(act):
                act.dma_start(dw_sb[:], w_dw.rearrange("(g i) a b c -> g i (a b c)", i=DIM)).then_inc(s_c, 16)
                act.dma_start(pw_sb[:], w_pw.rearrange("(g o) i -> g o i", o=DIM)).then_inc(s_c, 16)
                for n, a in enumerate((bn_gamma, bn_beta, bn_mean, bn_var)):
                    with nc.allow_non_contiguous_dma(reason="256 values"):
                        act.dma_start(bn_sb[:, n, :], a.rearrange("(t p) -> p t", p=P)).then_inc(s_b, 16)
                act.wait_ge(s_v, 3)
                nc.scalar.activation(bn_t[:, 1, :], bn_t[:, 0, :], ACT.Sqrt).then_inc(s_bn, 1)
                for n, job in enumerate(jobs):
                    act.wait_ge(s_tp, n + 1)
                    nc.scalar.activation(target(job, "hi"), ps[n % 4][:, 0:P], ACT.Copy).then_inc(s_hi, 1)

            @block.vector
            def _(dve):
                nc.vector.memset(kern[:].rearrange("g i o a b -> g (i o a b)"), 0.0).then_inc(s_v, 1)
                dve.wait_ge(s_v, 1)
                dve.wait_ge(s_c, 32)
                for ty in range(TAPS):
                    for tx in range(TAPS):
                        dw = dw_sb[:, :, ty * TAPS + tx:ty * TAPS + tx + 1].broadcast_to([G, DIM, DIM])
                        last = nc.vector.tensor_tensor(kern[:, :, :, ty + 3, tx + 3],
                                                       pw_sb[:].rearrange("g o i -> g i o"), dw, ALU.mult)
                last.then_inc(s_kern, 1)
                nc.vector.memset(keep["eps"][:], EPS).then_inc(s_v, 1)
                dve.wait_ge(s_b, 64)
                nc.vector.tensor_scalar_add(bn_t[:, 0, :], bn_sb[:, 3, :], BN_EPS).then_inc(s_v, 1)
                dve.wait_ge(s_bn, 1)
                nc.vector.reciprocal(bn_r[:], bn_t[:, 1, :]).then_inc(s_v, 1)
                dve.wait_ge(s_v, 4)
                nc.vector.tensor_tensor(bn_r[:], bn_r[:], bn_t[:, 0, :], ALU.mult).then_inc(s_v, 1)
                dve.wait_ge(s_v, 5)
                nc.vector.tensor_tensor(bn_r[:], bn_r[:], bn_t[:, 1, :], ALU.add).then_inc(s_v, 1)
                dve.wait_ge(s_v, 6)
                nc.vector.tensor_scalar_mul(bn_r[:], bn_r[:], 0.5).then_inc(s_v, 1)
                dve.wait_ge(s_v, 7)
                nc.vector.reciprocal(bn_t[:, 0, :], bn_r[:]).then_inc(s_v, 1)
                dve.wait_ge(s_v, 8)
                nc.vector.tensor_tensor(keep["bn_scale"][:], bn_sb[:, 0, :], bn_t[:, 0, :],
                                        ALU.mult).then_inc(s_v, 1)
                dve.wait_ge(s_v, 9)
                nc.vector.tensor_tensor(bn_t[:, 1, :], bn_sb[:, 2, :], keep["bn_scale"][:],
                                        ALU.mult).then_inc(s_v, 1)
                dve.wait_ge(s_v, 10)
                nc.vector.tensor_tensor(keep["bn_bias"][:], bn_sb[:, 1, :], bn_t[:, 1, :], ALU.subtract)
                for n, job in enumerate(jobs):
                    dve.wait_ge(s_hi, n + 1)
                    nc.vector.tensor_tensor(target(job, "lo"), ps[n % 4][:, 0:P],
                                            target(job, "hi").bitcast(F32), ALU.subtract).then_inc(s_lo, 1)

            @block.gpsimd
            def _(pool):
                for n, (t, value) in enumerate((("ident", 0.0), ("headmask", 1.0), ("planemask", 0.0),
                                                ("dimsel", 0.0))):
                    nc.gpsimd.memset(keep[t][:], value).then_inc(s_mask, 1)
                pool.wait_ge(s_mask, 4)
                sel = nc.gpsimd.affine_select
                sel(out=keep["ident"][:], in_=keep["ident"][:], compare_op=ALU.not_equal, fill=1.0, base=0,
                    pattern=[[-1, P]], channel_multiplier=1).then_inc(s_mask, 1)
                sel(out=keep["headmask"][:], in_=keep["headmask"][:], compare_op=ALU.is_ge, fill=0.0, base=0,
                    pattern=[[-DIM, HT]], channel_multiplier=1).then_inc(s_mask, 1)
                for k in range(DIM):
                    pool.wait_ge(s_mask, 6 + k)
                    sel(out=keep["planemask"][:], in_=keep["planemask"][:], compare_op=ALU.not_equal,
                        fill=1.0, base=-NPL * k, pattern=[[-1, NPL]], channel_multiplier=1).then_inc(s_mask, 1)
                pool.wait_ge(s_mask, 14)
                sel(out=keep["headmask"][:], in_=keep["headmask"][:], compare_op=ALU.is_ge, fill=0.0,
                    base=DIM - 1, pattern=[[DIM, HT]], channel_multiplier=-1).then_inc(s_mask, 1)
                for r in range(NPL):
                    pool.wait_ge(s_mask, 15 + r)
                    v = keep["dimsel"][:].rearrange("p (h d) -> p h d", d=DIM)
                    sel(out=v, in_=v, compare_op=ALU.not_equal, fill=1.0, base=-r,
                        pattern=[[0, HT], [-NPL, DIM]], channel_multiplier=1).then_inc(s_mask, 1)
                pool.wait_ge(s_mask, 15 + NPL)

            @block.tensor
            def _(pe):
                pe.wait_ge(s_w, 16 * (PARTS * KT + 1))
                pe.wait_ge(s_mask, 5)
                for n, job in enumerate(jobs):
                    if n >= 4:
                        pe.wait_ge(s_lo, n - 3)
                    nc.tensor.transpose(ps[n % 4][:, 0:P], source(job), keep["ident"][:]).then_inc(s_tp, 1)


def phase1_qkv(nc, keep, x_d, grid_d, q_d, n_batch):
    TILES = PARTS * KT
    NBK = NPIX // BANK
    NT = TILES * NBK
    UNITS = STG // (2 * P)
    assert (KT * UNITS) % 4 == 0 and STG - UNITS * 2 * P <= GS
    with ExitStack() as ctx:
        m = Mem(nc, ctx)
        xraw = m.sb("xraw", [P, KT, NPIX])
        xh = m.sb("xh", [P, KT, NPL, PLANE], F32R)
        xl = m.sb("xl", [P, KT, NPL, PLANE], F32R)
        stage = [m.sb(f"stage_{'qkv'[j]}", [P, NPL, GS, GS]) for j in range(PARTS)]
        qbuf = m.sb("qbuf", [P, NPL, PLANE])
        kh = m.sb("kh", [P, 4, 2, P], F32R)
        kl = m.sb("kl", [P, 4, 2, P], F32R)
        vt = m.sb("vt", [P, 4, 2, 2 * P + 2], F32R)
        vk_m = m.sb("vk_m", [P, DIM, 2 * HT])
        ps_qkv = [m.ps(f"ps_qkv{i}") for i in range(2)]
        ps_t = [m.ps(f"ps_t{i}") for i in range(4)]
        ps_vk = [m.ps(f"ps_vk{i}") for i in range(KT)]
        s_x = m.sem("x_loaded")
        s_zero = m.sem("borders_zeroed")
        s_xh = m.sem("xh_made")
        s_xl = m.sem("xl_made")
        s_mm = m.sem("qkv_bank_made")
        s_ev = [m.sem("even_bank_staged"), m.sem("odd_bank_staged")]
        s_q = m.sem("relu_q_made")
        s_tp = m.sem("unit_transposed")
        s_th = m.sem("unit_hi_made")
        s_tl = m.sem("unit_lo_made")
        s_vk = m.sem("unit_vk_made")
        s_acc = m.sem("vk_read")
        s_m = m.sem("vk_masked")
        s_st = [m.sem(f"stage_{'qkv'[j]}_stored") for j in range(PARTS)]
        s_qst = m.sem("relu_q_stored")
        LOADS = 16 * KT
        AHEAD = 2
        LAG = 3

        def x_view(kt, yo):
            v = xraw[:, kt, :].rearrange("p (by yo bx xo) -> p yo xo by bx", yo=PATCH, by=NB, bx=NB)
            return v[:, yo]

        def x_target(buf, kt, yo):
            return buf[:, kt, yo * PATCH:(yo + 1) * PATCH, :].rearrange("p a (b c) -> p a b c", c=NB)

        def shifted(j, bank):
            yo, xo = bank // 2, 2 * (bank % 2)
            yi, xi = (yo + 2) % PATCH, (xo + 2) % PATCH
            y0, x0 = int(yo >= 2), int(xo >= 2)
            return stage[j][:, yi * PATCH + xi:yi * PATCH + xi + 2, y0:y0 + NB, x0:x0 + NB]

        def planes(ap):
            return ap.rearrange("p (a b c) -> p a b c", b=NB, c=NB)

        def staged_wait(eng, b, n):
            eng.wait_ge(s_ev[n % 2], b * (NT // 2) + n // 2 + 2)

        def unit_tile(j, u, t):
            at = (2 * u + t) * P
            return stage[j][:].rearrange("p a b c -> p (a b c)")[:, at:at + P]

        def slot(half, u):
            return (half * UNITS + u) % 4

        with nc.Block() as block:
            @block.sync
            def _(sp):
                def load_x(b):
                    for kt in range(KT):
                        sp.dma_start(xraw[:, kt, :], x_d[b, kt * P:(kt + 1) * P, :]).then_inc(s_x, 16)

                def stores(b):
                    for t in range(TILES):
                        half, j = t // PARTS, t % PARTS
                        staged_wait(sp, b, t * NBK + NBK - 2)
                        staged_wait(sp, b, t * NBK + NBK - 1)
                        row = (j * KT + half) * P
                        sp.dma_start(grid_d[b, row:row + P, :],
                                     stage[j][:].rearrange("p a b c -> p (a b c)")).then_inc(s_st[j], 16)
                        if j == 0:
                            sp.wait_ge(s_q, b * (KT * NBK) + (half + 2) * NBK)
                            sp.dma_start(q_d[b, half * P:(half + 1) * P, :],
                                         qbuf[:].rearrange("p a b -> p (a b)")).then_inc(s_qst, 16)

                for j in range(PARTS):
                    sp.sem_inc(s_st[j], 16)
                sp.sem_inc(s_qst, 16)
                load_x(0)
                sp.wait_ge(s_zero, PARTS)
                with sp.Fori(0, n_batch - 1) as b:
                    sp.wait_ge(s_xh, b * (KT * PATCH) + KT * PATCH)
                    sp.wait_ge(s_xl, b * (KT * PATCH) + KT * PATCH)
                    load_x(b + 1)
                    stores(b)
                stores(n_batch - 1)
                for j in range(PARTS):
                    sp.wait_ge(s_st[j], 16 * (KT * n_batch + 1))
                sp.wait_ge(s_qst, 16 * (KT * n_batch + 1))

            @block.scalar
            def _(act):
                def split_hi(b, yo):
                    act.wait_ge(s_x, b * LOADS + LOADS)
                    for kt in range(KT):
                        nc.scalar.activation(x_target(xh, kt, yo), x_view(kt, yo), ACT.Copy).then_inc(s_xh, 1)

                def body(b, last):
                    for t in range(TILES):
                        half, j = t // PARTS, t % PARTS
                        act.wait_ge(s_st[j], (b * KT + half) * 16 + 16)
                        if j > 0:
                            act.wait_ge(s_tl, (b * KT + half) * UNITS + 4)
                        else:
                            act.wait_ge(s_q, (b * KT + half) * NBK + NBK)
                        for bank in range(0, NBK, 2):
                            n = t * NBK + bank
                            act.wait_ge(s_mm, b * NT + n + 1)
                            nc.scalar.activation(shifted(j, bank), planes(ps_qkv[0][:]),
                                                 ACT.Copy).then_inc(s_ev[0], 1)
                            if t == TILES - 1 and not last:
                                yo = bank // 2
                                act.wait_ge(s_mm, b * NT + n + 2)
                                split_hi(b + 1, yo)
                        if j == PARTS - 1:
                            chunk_hi(b, half)

                def chunk_hi(b, half):
                    for u in range(UNITS):
                        k = (b * KT + half) * UNITS + u
                        act.wait_ge(s_tp, k + 1)
                        act.wait_ge(s_vk, k + 1)
                        nc.scalar.activation(kh[:, slot(half, u)], ps_t[slot(half, u)][:, 0:2 * P].rearrange(
                            "p (a b) -> p a b", a=2), ACT.Relu)
                        nc.scalar.activation(vt[:, slot(half, u), :, P:2 * P], ps_t[slot(half, u)][:, 2 * P:].rearrange(
                            "p (a b) -> p a b", a=2), ACT.Copy).then_inc(s_th, 1)

                act.sem_inc(s_ev[0], 1)
                for yo in range(PATCH):
                    split_hi(0, yo)
                with act.Fori(0, n_batch - 1) as b:
                    body(b, False)
                body(n_batch - 1, True)

            @block.gpsimd
            def _(pool):
                def split_lo(b, yo):
                    pool.wait_ge(s_xh, b * (KT * PATCH) + KT * (yo + 1))
                    for kt in range(KT):
                        nc.gpsimd.tensor_tensor(x_target(xl, kt, yo), x_view(kt, yo),
                                                x_target(xh, kt, yo).bitcast(F32), ALU.subtract).then_inc(s_xl, 1)

                for j in range(PARTS):
                    nc.gpsimd.memset(stage[j][:].rearrange("p a b c -> p (a b c)"), 0.0).then_inc(s_zero, 1)
                nc.gpsimd.memset(vt[:, :, :, 2 * P:].bitcast(F32), 1.0).then_inc(s_zero, 1)
                for yo in range(PATCH):
                    split_lo(0, yo)
                with pool.Fori(0, n_batch - 1) as b:
                    for yo in range(PATCH):
                        split_lo(b + 1, yo)

            @block.vector
            def _(dve):
                def body(b):
                    for t in range(TILES):
                        half, j = t // PARTS, t % PARTS
                        dve.wait_ge(s_st[j], (b * KT + half) * 16 + 16)
                        if j == 0:
                            dve.wait_ge(s_qst, (b * KT + half) * 16 + 16)
                        for bank in range(1, NBK, 2):
                            n = t * NBK + bank
                            dve.wait_ge(s_mm, b * NT + n + 1)
                            nc.vector.tensor_copy(shifted(j, bank), planes(ps_qkv[1][:])).then_inc(s_ev[1], 1)
                            if j == 0:
                                staged_wait(dve, b, n - 1)
                                staged_wait(dve, b, n)
                                for k in (bank - 1, bank):
                                    nc.vector.tensor_scalar_max(
                                        planes(qbuf[:, 2 * k:2 * k + 2, :].rearrange("p a b -> p (a b)")),
                                        shifted(j, k), 0.0).then_inc(s_q, 1)
                        if j == PARTS - 1:
                            chunk_lo(b, half)

                def chunk_lo(b, half):
                    for u in range(UNITS):
                        dve.wait_ge(s_th, (b * KT + half) * UNITS + u + 1)
                        nc.vector.scalar_tensor_tensor(
                            kl[:, slot(half, u)], ps_t[slot(half, u)][:, 0:2 * P].rearrange("p (a b) -> p a b", a=2), 0.0,
                            kh[:, slot(half, u)].bitcast(F32), ALU.max, ALU.subtract)
                        nc.vector.tensor_tensor(
                            vt[:, slot(half, u), :, 0:P], ps_t[slot(half, u)][:, 2 * P:].rearrange("p (a b) -> p a b", a=2),
                            vt[:, slot(half, u), :, P:2 * P].bitcast(F32), ALU.subtract).then_inc(s_tl, 1)
                    dve.wait_ge(s_vk, (b * KT + half) * UNITS + UNITS + 4)
                    nc.vector.tensor_tensor(
                        vk_m[:].rearrange("p e (l h) -> p l e h", l=2),
                        ps_vk[half][:, 0:2 * P].rearrange("p (l h e) -> p l e h", l=2, e=DIM),
                        keep["headmask"][:].rearrange("p (l e h) -> p l e h", l=1, e=1
                                                      ).broadcast_to([P, 2, DIM, HT]),
                        ALU.mult).then_inc(s_m, 1)
                    nc.vector.tensor_copy(keep["vk_a"][:, b, half, DIM:],
                                          ps_vk[half][:, 2 * P:2 * P + 1]).then_inc(s_acc, 1)
                    dve.wait_ge(s_m, b * KT + half + 1)
                    nc.vector.tensor_reduce(keep["vk_a"][:, b, half, 0:DIM], vk_m[:], AX_X, ALU.add)

                dve.sem_inc(s_ev[1], 1)
                dve.sem_inc(s_q, NBK)
                dve.sem_inc(s_tl, 4)
                dve.sem_inc(s_acc, KT)
                dve.wait_ge(s_zero, PARTS + 1)
                with dve.Fori(0, n_batch) as b:
                    body(b)

            @block.tensor
            def _(pe):
                def tile_banks(b, t, banks):
                    for bank in banks:
                        n = t * NBK + bank
                        if t == 0 and bank % 2 == 0:
                            yo = bank // 2
                            pe.wait_ge(s_xh, b * (KT * PATCH) + KT * (yo + 1))
                            pe.wait_ge(s_xl, b * (KT * PATCH) + KT * (yo + 1))
                        pe.wait_ge(s_ev[n % 2], b * (NT // 2) + n // 2 + 1)
                        col = (t % PARTS) * KT + t // PARTS
                        k = 0
                        for kt in range(KT):
                            ws = [keep[w][:, kt, col * P:(col + 1) * P] for w in ("wq_hi", "wq_lo")]
                            xs = [v[:, kt, 2 * bank:2 * bank + 2, :] for v in (xh, xl)]
                            for w, mv in split_passes(ws[0], ws[1], xs[0], xs[1]):
                                last = nc.tensor.matmul(ps_qkv[n % 2][:], w, mv, start=(k == 0),
                                                        stop=(k == PARTS * KT - 1))
                                k += 1
                        last.then_inc(s_mm, 1)

                def transposes(b, half, u):
                    pe.wait_ge(s_tl, (b * KT + half) * UNITS + u + 1)
                    for j in (1, 2):
                        for t in range(2):
                            c = ((j - 1) * 2 + t) * P
                            last = nc.tensor.transpose(ps_t[slot(half, u)][:, c:c + P], unit_tile(j, u, t),
                                                       keep["ident"][:])
                    last.then_inc(s_tp, 1)

                def vk(b, half, u):
                    if u == 0:
                        pe.wait_ge(s_acc, b * KT + half + 1)
                    pe.wait_ge(s_tl, (b * KT + half) * UNITS + u + 5)
                    for t in range(2):
                        v = vt[:, slot(half, u), t]
                        nc.tensor.matmul(ps_vk[half][:, 0:2 * P + 2], kh[:, slot(half, u), t], v,
                                         start=(u == 0 and t == 0), stop=False)
                        last = nc.tensor.matmul(ps_vk[half][:, P:2 * P + 2], kl[:, slot(half, u), t], v[:, P:],
                                                start=False, stop=(u == UNITS - 1 and t == 1))
                    last.then_inc(s_vk, 1)

                def chunk(b, half, between):
                    between(0)
                    for n in (NBK - 2, NBK - 1):
                        staged_wait(pe, b, (half * PARTS + 2) * NBK + n)
                    for u in range(LAG):
                        transposes(b, half, u)
                    between(1)
                    for u in range(LAG, UNITS + LAG):
                        if u < UNITS:
                            transposes(b, half, u)
                        vk(b, half, u - LAG)

                def body(b, last):
                    for half in range(KT):
                        for j in range(PARTS):
                            tile_banks(b, half * PARTS + j, range(AHEAD if j == 0 else 0, NBK))
                        nb, nt = (b, PARTS) if half == 0 else (b + 1, 0)
                        if half == 0 or not last:
                            chunk(b, half, lambda n: tile_banks(nb, nt, (n,)))
                        else:
                            chunk(b, half, lambda n: None)

                pe.sem_inc(s_vk, 4)
                pe.wait_ge(s_zero, PARTS + 1)
                tile_banks(0, 0, range(AHEAD))
                with pe.Fori(0, n_batch - 1) as b:
                    body(b, False)
                body(n_batch - 1, True)


def kept(nc, ctx, n_batch):
    m = Mem(nc, ctx)
    return {
        "wp_hi": m.sb("wp_hi", [P, 2 * KT, C], F32R), "wp_lo": m.sb("wp_lo", [P, 2 * KT, C], F32R),
        "ident": m.sb("ident", [P, P]), "headmask": m.sb("headmask", [P, HT]),
        "planemask": m.sb("planemask", [P, NPL]), "dimsel": m.sb("dimsel", [P, P]),
        "bn_scale": m.sb("bn_scale", [P, KT]), "bn_bias": m.sb("bn_bias", [P, KT]),
        "eps": m.sb("eps", [P, 1]),
        "vk_a": m.sb("vk_a", [P, n_batch, KT, DIM + 1]),
    }


def phase2_agg(nc, keep, kern_d, grid_d, q_d, n_batch, n_heads):
    NPAIR = n_batch // 2
    SLOTS = PARTS * NPAIR
    UNITS = 2 * NPAIR
    CH = 4
    CHUNKS = PARTS * n_batch // CH
    RING = 3
    PART = (1, 2, 0)
    assert n_batch % CH == 0 and SLOTS % RING == 0 and CHUNKS % RING == 0
    with ExitStack() as ctx:
        m = Mem(nc, ctx)
        xin = [m.sb(f"grid_in{i}", [P, CH, GS, GS]) for i in range(RING)]
        gh = [m.sb(f"grid_hi{i}", [P, 2, GS, GS], F32R) for i in range(RING)]
        gl = [m.sb(f"grid_lo{i}", [P, 2, GS, GS], F32R) for i in range(RING)]
        win = [m.sb(f"window{jj}", [P, KROW]) for jj in range(PARTS)]
        bh = [m.sb(f"band_hi{jj}", [P, 4, DIM, PATCH, PATCH], F32R) for jj in range(PARTS)]
        bl = [m.sb(f"band_lo{jj}", [P, 4, DIM, PATCH, PATCH], F32R) for jj in range(PARTS)]
        kvf = [m.sb(f"kv_agg{i}", [P, BANK]) for i in range(3)]
        qf = [m.sb(f"q_agg{i}", [P, 2, PLANE]) for i in range(2)]
        kth = m.sb("kt_hi", [P, NPAIR, 4, P], F32R)
        ktl = m.sb("kt_lo", [P, NPAIR, 4, P], F32R)
        vt = m.sb("vt_lo_hi", [P, 2, 4, 2, P], F32R)
        vk_m = m.sb("vkb_m", [P, 2, 2, DIM, 2 * NPL])
        ps_c = [m.ps(f"ps_conv{i}") for i in range(RING)]
        ps_t = [m.ps(f"ps_tr{i}") for i in range(2)]
        ps_vk = [m.ps(f"ps_vkb{i}") for i in range(2)]
        s_in = [m.sem(f"grid_in{i}_loaded") for i in range(RING)]
        s_gh = m.sem("grid_hi_made")
        s_gl = m.sem("grid_lo_made")
        s_win = [m.sem(f"window{jj}_loaded") for jj in range(PARTS)]
        s_bhi = m.sem("bands_hi_made")
        s_band = m.sem("bands_made")
        s_conv = m.sem("conv_made")
        s_ev = m.sem("conv_read")
        s_tp = m.sem("agg_transposed")
        s_th = m.sem("agg_hi_made")
        s_tl = m.sem("agg_lo_made")
        s_vk = m.sem("vkb_made")
        s_g = m.sem("vkb_read")
        s_gm = m.sem("vkb_first_masked")
        s_ks = m.sem("ksum_made")
        s_qst = [m.sem(f"q_agg{i}_stored") for i in range(2)]

        def quadrants(jj):
            w = win[jj][:].rearrange("p (o u w) -> p o u w", o=DIM, u=PADK)
            for a in range(2):
                for b in range(2):
                    us = slice(4 * a + 3, 4 * a - 1 if a else None, -1)
                    ws = slice(4 * b + 3, 4 * b - 1 if b else None, -1)
                    yield 2 * a + b, w[:, :, us, ws]

        with nc.Block() as block:
            @block.sync
            def _(sp):
                def load_grid(h, c):
                    jj, part = c * CH // n_batch, c % (n_batch // CH)
                    sp.wait_ge(s_gl, h * SLOTS + 2 * c + 2)
                    row = (h + PART[jj] * HEADS) * DIM
                    src = grid_d[part * CH:(part + 1) * CH, bass.ds(row, DIM), :]
                    sp.dma_start(xin[c % RING][:].rearrange("p b y x -> p b (y x)"),
                                 src.rearrange("b i (k n) -> (i k) b n", n=GRID)).then_inc(s_in[c % RING], 16)

                def load_window(h, jj):
                    for i in range(DIM):
                        row = kern_d[h * PARTS + PART[jj], i]
                        src = bass.AP(tensor=row.tensor, offset=row.offset,
                                      ap=[[PADK, PATCH], [1, PATCH], [1, RWIN]])
                        sp.dma_start(win[jj][i * NPL:(i + 1) * NPL, 0:RWIN], src).then_inc(s_win[jj], 16)

                def body(h, last):
                    for c in range(CHUNKS):
                        load_grid(h, c)
                        for jj in range(PARTS):
                            if c == min((jj + 1) * CHUNKS // PARTS, CHUNKS - 1) and not last:
                                sp.wait_ge(s_band, h * PARTS + jj + 1)
                                load_window(h + 1, jj)

                for jj in range(PARTS):
                    load_window(0, jj)
                with sp.Fori(0, n_heads - 1) as h:
                    body(h, False)
                body(n_heads - 1, True)

            @block.gpsimd
            def _(pool):
                def band_lo(h, jj):
                    pool.wait_ge(s_bhi, h * PARTS + jj + 1)
                    for n, taps in quadrants(jj):
                        last = nc.gpsimd.tensor_tensor(bl[jj][:, n], taps, bh[jj][:, n].bitcast(F32),
                                                       ALU.subtract)
                    last.then_inc(s_band, 1)

                def grid_lo(h, s):
                    pool.wait_ge(s_gh, h * SLOTS + s + 1)
                    s = s % SLOTS
                    c, half = s // 2, s % 2
                    nc.gpsimd.tensor_tensor(
                        gl[s % RING][:].rearrange("p b y x -> p (b y x)"),
                        xin[c % RING][:, 2 * half:2 * half + 2].rearrange("p b y x -> p (b y x)"),
                        gh[s % RING][:].rearrange("p b y x -> p (b y x)").bitcast(F32),
                        ALU.subtract).then_inc(s_gl, 1)

                def body(h, last):
                    for s in range(SLOTS):
                        if s + 2 < SLOTS or not last:
                            grid_lo(h, s + 2)
                        if s == 1:
                            band_lo(h, 2)
                        for jj in (0, 1):
                            if s == (jj + 1) * NPAIR and not last:
                                band_lo(h + 1, jj)

                pool.sem_inc(s_gl, 2 * RING)
                band_lo(0, 0)
                band_lo(0, 1)
                grid_lo(0, 0)
                grid_lo(0, 1)
                with pool.Fori(0, n_heads - 1) as h:
                    body(h, False)
                body(n_heads - 1, True)

            @block.vector
            def _(dve):
                def grid_hi(h, s):
                    dve.wait_ge(s_conv, h * SLOTS + s + 1)
                    wrap, s = s // SLOTS, s % SLOTS
                    c, half = s // 2, s % 2
                    dve.wait_ge(s_in[c % RING], (h + wrap) * (16 * CHUNKS // RING) + 16 * (c // RING + 1))
                    nc.vector.tensor_copy(gh[s % RING][:].rearrange("p b y x -> p (b y x)"),
                                          xin[c % RING][:, 2 * half:2 * half + 2].rearrange("p b y x -> p (b y x)")
                                          ).then_inc(s_gh, 1)

                def band_hi(h, jj):
                    dve.wait_ge(s_win[jj], h * (16 * DIM) + 16 * DIM)
                    for n, taps in quadrants(jj):
                        last = nc.vector.tensor_copy(bh[jj][:, n], taps)
                    last.then_inc(s_bhi, 1)

                def unit_lo(h, u):
                    pair = u % NPAIR
                    dve.wait_ge(s_th, h * UNITS + u + 1)
                    src = ps_t[u % 2][:].rearrange("p (a n) -> p a n", n=P)
                    if u < NPAIR:
                        hi, lo = kth[:, pair], ktl[:, pair]
                    else:
                        hi, lo = vt[:, pair % 2, :, 1], vt[:, pair % 2, :, 0]
                    nc.vector.tensor_tensor(lo, src, hi.bitcast(F32), ALU.subtract).then_inc(s_tl, 1)

                def ksum(h, pair):
                    dve.wait_ge(s_ev, h * SLOTS + pair + 4)
                    nc.vector.tensor_reduce(keep["vk_b"][:, 2 * pair:2 * pair + 2, bass.ds(h, 1), DIM],
                                            kvf[pair % 3][:].rearrange("p (b n) -> p b n", b=2),
                                            AX_X, ALU.add).then_inc(s_ks, 1)

                def collect(h, pair):
                    dve.wait_ge(s_vk, h * NPAIR + pair + 1 + NPAIR)
                    v = ps_vk[pair % 2][:].rearrange("p (b l e k) -> p b l e k", b=2, l=2, k=NPL)
                    for b in range(2):
                        nc.vector.tensor_tensor(
                            vk_m[:, pair % 2, b].rearrange("p e (l k) -> p l e k", l=2), v[:, b],
                            keep["planemask"][:].rearrange("p (l e k) -> p l e k", l=1, e=1
                                                           ).broadcast_to([P, 2, DIM, NPL]),
                            ALU.mult).then_inc(s_gm if b == 0 else s_g, 1)
                    dve.wait_ge(s_g, h * NPAIR + pair + 3)
                    nc.vector.tensor_reduce(
                        keep["vk_b"][:, 2 * pair:2 * pair + 2, bass.ds(h, 1), 0:DIM],
                        vk_m[:, pair % 2], AX_X, ALU.add)

                def body(h, last):
                    for s in range(SLOTS):
                        if s + 2 < SLOTS or not last:
                            grid_hi(h, s + 2)
                        if s == 1:
                            dve.wait_ge(s_conv, h * SLOTS + 3)
                            band_hi(h, 2)
                        for jj in (0, 1):
                            if s == (jj + 1) * NPAIR and not last:
                                dve.wait_ge(s_conv, h * SLOTS + (jj + 1) * NPAIR + 3)
                                band_hi(h + 1, jj)
                        if s < NPAIR:
                            ksum(h, s)
                        if 2 <= s < UNITS + 2:
                            unit_lo(h, s - 2)
                        if NPAIR + 3 <= s < UNITS + 3:
                            collect(h, s - NPAIR - 3)

                dve.sem_inc(s_tl, 2)
                dve.sem_inc(s_g, 2)
                dve.sem_inc(s_ks, 3)
                band_hi(0, 0)
                band_hi(0, 1)
                grid_hi(0, 0)
                grid_hi(0, 1)
                with dve.Fori(0, n_heads - 1) as h:
                    body(h, False)
                body(n_heads - 1, True)

            @block.scalar
            def _(act):
                def read_conv(h, s):
                    jj, pair = s // NPAIR, s % NPAIR
                    act.wait_ge(s_conv, h * SLOTS + s + 4)
                    if jj < 2:
                        act.wait_ge(s_tp, h * UNITS + max(s, 2))
                        act.wait_ge(s_ks, h * NPAIR + min(max(s + 1, 3), NPAIR + 3))
                        nc.scalar.activation(kvf[s % 3][:], ps_c[s % RING][:],
                                             ACT.Relu if jj == 0 else ACT.Copy).then_inc(s_ev, 1)
                    else:
                        act.wait_ge(s_qst[pair % 2], h * (16 * NPAIR // 2) + 16 * (pair // 2 + 1))
                        nc.scalar.activation(qf[pair % 2][:].rearrange("p b n -> p (b n)"), ps_c[s % RING][:],
                                             ACT.Relu).then_inc(s_ev, 1)

                def store_q(h, pair):
                    act.wait_ge(s_ev, h * SLOTS + 2 * NPAIR + pair + 4)
                    dst = q_d[2 * pair:2 * pair + 2, bass.ds(C + h * DIM, DIM), :]
                    act.dma_start(dst.rearrange("b o (k n) -> (o k) b n", n=PLANE),
                                  qf[pair % 2][:]).then_inc(s_qst[pair % 2], 16)

                def unit_hi(h, u):
                    pair = u % NPAIR
                    act.wait_ge(s_tp, h * UNITS + u + 3)
                    src = ps_t[u % 2][:].rearrange("p (a n) -> p a n", n=P)
                    if u < NPAIR:
                        act.wait_ge(s_vk, h * NPAIR + pair + 1)
                        dst = kth[:, pair]
                    else:
                        act.wait_ge(s_vk, h * NPAIR + pair - 1 + NPAIR)
                        dst = vt[:, pair % 2, :, 1]
                    nc.scalar.activation(dst, src, ACT.Copy).then_inc(s_th, 1)

                def body(h):
                    for s in range(SLOTS):
                        read_conv(h, s)
                        if 2 <= s < UNITS + 2:
                            unit_hi(h, s - 2)
                        if s > 2 * NPAIR:
                            store_q(h, s - 2 * NPAIR - 1)
                    store_q(h, NPAIR - 1)

                act.sem_inc(s_ev, RING)
                for i in range(2):
                    act.sem_inc(s_qst[i], 16)
                with act.Fori(0, n_heads) as h:
                    body(h)
                for i in range(2):
                    act.wait_ge(s_qst[i], 16 * (n_heads * NPAIR // 2 + 1))

            @block.tensor
            def _(pe):
                def conv(h, s):
                    jj = s // NPAIR
                    if s % NPAIR == 0:
                        pe.wait_ge(s_band, h * PARTS + jj + 1)
                    pe.wait_ge(s_gl, h * SLOTS + s + 1 + 2 * RING)
                    pe.wait_ge(s_ev, h * SLOTS + s + 1)
                    k = 0
                    for a in range(2):
                        for b in range(2):
                            ws = [v[jj][:, 2 * a + b].rearrange("p o y x -> p (o y x)") for v in (bh, bl)]
                            xs = [v[s % RING][:, :, a:a + NB, b:b + NB] for v in (gh, gl)]
                            for w, mv in split_passes(ws[0], ws[1], xs[0], xs[1]):
                                last = nc.tensor.matmul(ps_c[s % RING][:], w, mv, start=(k == 0), stop=(k == 11))
                                k += 1
                    last.then_inc(s_conv, 1)

                def transposes(h, u):
                    pe.wait_ge(s_ev, h * SLOTS + u + 4)
                    pe.wait_ge(s_tl, h * UNITS + u + 1)
                    for t in range(4):
                        last = nc.tensor.transpose(ps_t[u % 2][:, t * P:(t + 1) * P],
                                                   kvf[u % 3][:, t * P:(t + 1) * P], keep["ident"][:])
                    last.then_inc(s_tp, 1)

                def vk(h, pair):
                    pe.wait_ge(s_tl, h * UNITS + NPAIR + pair + 3)
                    pe.wait_ge(s_g, h * NPAIR + pair + 1)
                    for b in range(2):
                        out = ps_vk[pair % 2][:, b * 2 * P:(b + 1) * 2 * P]
                        for t in range(2):
                            v = vt[:, pair % 2, 2 * b + t]
                            nc.tensor.matmul(out, kth[:, pair, 2 * b + t], v.rearrange("p l n -> p (l n)"),
                                             start=(t == 0), stop=False)
                            last = nc.tensor.matmul(out[:, P:], ktl[:, pair, 2 * b + t], v[:, 1],
                                                    start=False, stop=(t == 1))
                    last.then_inc(s_vk, 1)

                pe.sem_inc(s_conv, RING)
                pe.sem_inc(s_tp, 2)
                pe.sem_inc(s_vk, NPAIR)
                with pe.Fori(0, n_heads) as h:
                    for s in range(SLOTS):
                        conv(h, s)
                        if 2 <= s < UNITS + 2:
                            transposes(h, s - 2)
                        if NPAIR + 3 <= s < UNITS + 3:
                            vk(h, s - NPAIR - 3)


def phase3_out(nc, keep, x_d, q_d, out_d, n_batch):
    T = 2 * KT
    CHUNKS = NPIX // BANK
    PAIRS = CHUNKS // 2
    NH2 = 2 * HEADS
    RING = 4
    HALF = CHUNKS // 2
    with ExitStack() as ctx:
        m = Mem(nc, ctx)
        qraw = [m.sb(f"q_raw{i}", [P, T, BANK]) for i in range(RING)]
        qh = [m.sb(f"q_hi{i}", [P, T, BANK], F32R) for i in range(2)]
        ql = [m.sb(f"q_lo{i}", [P, T, BANK], F32R) for i in range(2)]
        qn = [m.sb(f"q_norm{i}", [P, BANK]) for i in range(T)]
        nh = [m.sb(f"q_norm_hi{i}", [P, T, BANK], F32R) for i in range(2)]
        nl = [m.sb(f"q_norm_lo{i}", [P, T, BANK], F32R) for i in range(2)]
        xy = [m.sb(f"x_half{i}", [P, KT, NPIX // 2]) for i in range(2)]
        ybn = [m.sb(f"y_bn{i}", [P, BANK]) for i in range(2)]
        mth = [m.sb(f"mt_hi{i}", [P, T, C], F32R) for i in range(2)]
        mtl = [m.sb(f"mt_lo{i}", [P, T, C], F32R) for i in range(2)]
        sdh = m.sb("sden_hi", [P, T, 3 * NH2], F32R)
        sdl = m.sb("sden_lo", [P, T, 3 * NH2], F32R)
        sd = m.sb("sden", [P, T, HT])
        vkd = m.sb("vk_diag", [P, T, P])
        vkh = m.sb("vk_t_hi", [P, T, P], F32R)
        vkl = m.sb("vk_t_lo", [P, T, P], F32R)
        den = m.sb("den", [P, BANK])
        rec = [m.sb(f"rec_hl{i}", [P, BANK], F32R) for i in range(2)]
        spread_f = vkd
        spread = m.sb("spread", [P, T, P], F32R)
        ps_den = m.ps("ps_den")
        ps_r = [m.ps(f"ps_rec{i}") for i in range(2)]
        ps_y = [m.ps(f"ps_y{i}") for i in range(KT)]
        ps_p = [m.ps(f"ps_prep{i}") for i in range(2)]
        s_q = [m.sem(f"q_raw{i}_loaded") for i in range(RING)]
        s_x = [m.sem(f"x_half{i}_loaded") for i in range(2)]
        s_out = [m.sem(f"y_half{i}_stored") for i in range(2)]
        s_c = m.sem("spread_step")
        s_z = m.sem("sden_zeroed")
        s_qh = m.sem("q_hi_made")
        s_ql = m.sem("q_lo_made")
        s_den = m.sem("den_made")
        s_de = m.sem("den_eps_made")
        s_rc = m.sem("den_inverted")
        s_rh = m.sem("rec_hi_made")
        s_rl = m.sem("rec_lo_made")
        s_r = m.sem("rec_spread")
        s_n = m.sem("q_norm_made")
        s_nh = m.sem("q_norm_hi_made")
        s_nl = m.sem("q_norm_lo_made")
        s_y = m.sem("y_made")
        s_bn = m.sem("y_bn_made")
        s_add = m.sem("y_added")
        s_p1 = m.sem("prep_sums_made")
        s_p2 = m.sem("prep_diag_made")
        s_sf = m.sem("prep_sden_made")
        s_sh = m.sem("prep_sden_hi_made")
        s_sl = m.sem("prep_sden_lo_made")
        s_p3 = m.sem("prep_transposed")
        s_p4 = m.sem("prep_vk_hi_made")
        s_p5 = m.sem("prep_vk_lo_made")
        s_p6 = m.sem("prep_mt_made")
        s_p7 = m.sem("prep_mt_hi_made")
        s_p8 = m.sem("prep_mt_lo_made")

        def stored_half(buf, half, kt):
            v = buf[kt * P:(kt + 1) * P, :].rearrange("p (by yo x) -> p by yo x", yo=PATCH, x=W)
            return v[:, :, 2 * half:2 * half + 2, :]

        def chunk_of_half(g, kt, c):
            yo, xo = (c // 2) % 2, 2 * (c % 2)
            v = xy[g][:, kt, :].rearrange("p (by yo bx xo) -> p yo xo by bx", yo=2, by=NB, bx=NB)
            return v[:, yo, xo:xo + 2]

        def heads_mask(n):
            return keep["headmask"][:].rearrange("p (h a) -> p h a", a=1).broadcast_to([P, HT, n])

        def by_batch(eng, body):
            with eng.Fori(0, n_batch // 2 - 1) as i:
                body(i * 2, False, 0)
                body(i * 2 + 1, False, 1)
            body(n_batch - 2, False, 0)
            body(n_batch - 1, True, 1)

        with nc.Block() as block:
            @block.sync
            def _(sp):
                def load_q(b, c):
                    sp.wait_ge(s_n, (b * CHUNKS + c - RING + 1) * T + 2)
                    src = q_d[b, :, c * BANK:(c + 1) * BANK].rearrange("(t p) n -> p t n", p=P)
                    sp.dma_start(qraw[c % RING][:], src).then_inc(s_q[c % RING], 16)

                def load_x(b, half):
                    for kt in range(KT):
                        sp.dma_start(xy[half][:, kt, :].rearrange("p (by yo x) -> p by yo x", by=NB, yo=2),
                                     stored_half(x_d[b], half, kt)).then_inc(s_x[half], 16)

                def load_pair(b, J):
                    for c in (2 * J + RING, 2 * J + RING + 1):
                        if c < CHUNKS:
                            load_q(b, c)
                        else:
                            load_q(b + 1, c - CHUNKS)

                def body(b, last, par):
                    for J in range(1, PAIRS):
                        if 2 * J + RING < CHUNKS or not last:
                            load_pair(b, J)
                        if J == PAIRS // 2 and not last:
                            sp.wait_ge(s_out[0], b * (16 * KT) + 16 * KT)
                            load_x(b + 1, 0)
                    if not last:
                        load_pair(b + 1, 0)
                        sp.wait_ge(s_out[1], b * (16 * KT) + 16 * KT)
                        load_x(b + 1, 1)

                for c in range(RING):
                    src = q_d[0, :, c * BANK:(c + 1) * BANK].rearrange("(t p) n -> p t n", p=P)
                    sp.dma_start(qraw[c][:], src).then_inc(s_q[c], 16)
                for half in range(2):
                    load_x(0, half)
                load_pair(0, 0)
                by_batch(sp, body)

            def raw_loaded(eng, b, c):
                eng.wait_ge(s_q[c % RING], b * (16 * CHUNKS // RING) + 16 * (c // RING + 1))

            @block.gpsimd
            def _(pool):
                def q_lo(b, c):
                    for t in range(T):
                        pool.wait_ge(s_qh, (b * CHUNKS + c) * T + t + 1)
                        nc.gpsimd.tensor_tensor(ql[c % 2][:, t], qraw[c % RING][:, t],
                                                qh[c % 2][:, t].bitcast(F32), ALU.subtract).then_inc(s_ql, 1)

                def add_x(b, c):
                    for kt in range(KT):
                        half = c // HALF
                        pool.wait_ge(s_x[half], b * (16 * KT) + 16 * KT)
                        pool.wait_ge(s_bn, (b * CHUNKS + c) * KT + kt + 3)
                        v = chunk_of_half(half, kt, c)
                        nc.gpsimd.tensor_tensor(v, ybn[kt][:].rearrange("p (a b c) -> p a b c", a=2, b=NB),
                                                v, ALU.add).then_inc(s_add, 1)

                def store(b, half):
                    pool.wait_ge(s_add, (b * CHUNKS + (half + 1) * HALF) * KT + 2)
                    for kt in range(KT):
                        pool.dma_start(stored_half(out_d[b], half, kt),
                                       xy[half][:, kt, :].rearrange("p (by yo x) -> p by yo x", by=NB, yo=2)
                                       ).then_inc(s_out[half], 16)

                def body(b, last, par):
                    for J in range(PAIRS):
                        for k in range(2):
                            c = 2 * J + RING + k
                            if c < CHUNKS or not last:
                                q_lo(b, c)
                            add_x(b, 2 * J + k)
                        if J % 2:
                            store(b, J // 2)

                pool.sem_inc(s_add, 2)
                nc.gpsimd.memset(spread_f[:], 0.0).then_inc(s_c, 1)
                for s in range(2):
                    pool.wait_ge(s_c, s + 1)
                    for t in range(T):
                        v = spread_f[:, t].rearrange("p (h e) -> p h e", e=DIM)
                        last = nc.gpsimd.affine_select(
                            out=v, in_=v, compare_op=ALU.not_equal, fill=1.0, base=-NH2 * s - HT * t,
                            pattern=[[-1, HT], [0, DIM]], channel_multiplier=1)
                    last.then_inc(s_c, 1)
                for c in range(4):
                    q_lo(0, c)
                by_batch(pool, body)
                for h in range(2):
                    pool.wait_ge(s_out[h], 16 * KT * n_batch)

            @block.scalar
            def _(act):
                def q_hi(b, c):
                    act.wait_ge(s_den, b * PAIRS + c // 2 + 1)
                    raw_loaded(act, b, c)
                    for t in range(T):
                        nc.scalar.activation(qh[c % 2][:, t], qraw[c % RING][:, t], ACT.Copy).then_inc(s_qh, 1)

                def den_eps(b, J):
                    act.wait_ge(s_den, b * PAIRS + J + 2)
                    act.wait_ge(s_rl, (b * PAIRS + J) * 2 + 1)
                    nc.scalar.activation(den[:], ps_den[:], ACT.Identity, bias=keep["eps"][:]).then_inc(s_de, 1)

                def rec_hi(b, J):
                    act.wait_ge(s_rc, b * PAIRS + J + 1)
                    act.wait_ge(s_r, (b * PAIRS + J) * (2 * T) + 1)
                    for k in range(2):
                        at = slice(k * NH2, (k + 1) * NH2)
                        nc.scalar.activation(rec[k][at, :], den[at, :], ACT.Copy).then_inc(s_rh, 1)

                def norm_hi(b, c, t):
                    if t == 0:
                        act.wait_ge(s_y, (b * CHUNKS + c) * KT + 2)
                    act.wait_ge(s_n, (b * CHUNKS + c) * T + t + 3)
                    nc.scalar.activation(nh[c % 2][:, t], qn[t][:], ACT.Copy).then_inc(s_nh, 1)

                def bn(b, c, kts):
                    for kt in kts:
                        act.wait_ge(s_y, (b * CHUNKS + c) * KT + kt + 5)
                        act.wait_ge(s_add, (b * CHUNKS + c) * KT + kt + 1)
                        nc.scalar.activation(ybn[kt][:], ps_y[kt][:], ACT.Identity,
                                             bias=keep["bn_bias"][:, kt:kt + 1],
                                             scale=keep["bn_scale"][:, kt:kt + 1]).then_inc(s_bn, 1)

                def vk_hi(b):
                    act.wait_ge(s_p3, b + 1)
                    nc.scalar.activation(vkh[:].rearrange("p t n -> p (t n)"), ps_p[1][:],
                                         ACT.Copy).then_inc(s_p4, 1)

                def mt_hi(b, par, bank):
                    act.wait_ge(s_p6, b * 2 + bank + 1)
                    nc.scalar.activation(mth[par][:, 2 * bank:2 * bank + 2, :].rearrange("p t n -> p (t n)"),
                                         ps_p[bank][:], ACT.Copy).then_inc(s_p7, 1)

                def body(b, last, par):
                    for J in range(PAIRS):
                        for t in range(T):
                            norm_hi(b, 2 * J + 1, t)
                        ahead = J + 1 < PAIRS or not last
                        more = 2 * J + RING < CHUNKS or not last
                        if ahead:
                            den_eps(b, J + 1)
                        if more:
                            q_hi(b, 2 * J + RING)
                        bn(b, 2 * J, (0,))
                        if more:
                            q_hi(b, 2 * J + RING + 1)
                        if ahead:
                            rec_hi(b, J + 1)
                        bn(b, 2 * J, (1,))
                        if ahead:
                            for t in range(T):
                                norm_hi(b, 2 * J + 2, t)
                        bn(b, 2 * J + 1, range(KT))
                        if J == 1 and not last:
                            vk_hi(b + 1)
                        if J == 2 and not last:
                            for bank in range(2):
                                mt_hi(b + 1, 1 - par, bank)

                act.sem_inc(s_bn, 2)
                for k in range(2):
                    q_hi(0, k)
                vk_hi(0)
                for bank in range(2):
                    mt_hi(0, 0, bank)
                den_eps(0, 0)
                rec_hi(0, 0)
                for k in range(2):
                    q_hi(0, 2 + k)
                for t in range(T):
                    norm_hi(0, 0, t)
                by_batch(act, body)

            @block.vector
            def _(dve):
                def norms(b, c):
                    n = (b * CHUNKS + c) * T

                    def product(t):
                        dve.wait_ge(s_r, n + t + 2)
                        nc.vector.tensor_tensor(qn[t][:], qraw[c % RING][:, t], ps_r[t % 2][:],
                                                ALU.mult).then_inc(s_n, 1)

                    def low(t):
                        dve.wait_ge(s_nh, n + t + 1)
                        nc.vector.tensor_tensor(nl[c % 2][:, t], qn[t][:], nh[c % 2][:, t].bitcast(F32),
                                                ALU.subtract).then_inc(s_nl, 1)

                    product(0)
                    for t in range(1, T):
                        product(t)
                        low(t - 1)
                    low(T - 1)

                def invert(b, J):
                    dve.wait_ge(s_de, b * PAIRS + J + 1)
                    nc.vector.reciprocal(den[:], den[:]).then_inc(s_rc, 1)
                    for k in range(2):
                        at, other = slice(k * NH2, (k + 1) * NH2), slice((1 - k) * NH2, (2 - k) * NH2)
                        dve.wait_ge(s_rh, (b * PAIRS + J) * 2 + k + 1)
                        nc.vector.tensor_tensor(rec[k][other, :], den[at, :], rec[k][at, :].bitcast(F32),
                                                ALU.subtract).then_inc(s_rl, 1)

                def prep_diag(b):
                    dve.wait_ge(s_p1, b + 1)
                    sums = ps_p[0][:, 0:KT * HT * (DIM + 1)].rearrange("p (t h e) -> p t h e", t=KT, h=HT)
                    for t in range(T):
                        if t < KT:
                            vk = keep["vk_a"][:, bass.ds(b, 1), t, 0:DIM].broadcast_to([P, HT, DIM])
                        else:
                            vk = sums[:, t - KT, :, 0:DIM]
                        last = nc.vector.tensor_tensor(vkd[:, t].rearrange("p (h e) -> p h e", e=DIM), vk,
                                                       heads_mask(DIM), ALU.mult)
                    last.then_inc(s_p2, 1)
                    for t in range(T):
                        if t < KT:
                            ks = keep["vk_a"][:, bass.ds(b, 1), t, DIM:].rearrange("p a e -> p (a e)"
                                                                                ).broadcast_to([P, HT])
                        else:
                            ks = sums[:, t - KT, :, DIM]
                        last = nc.vector.tensor_tensor(sd[:, t], ks, keep["headmask"][:], ALU.mult)
                    last.then_inc(s_sf, 1)

                def prep_sden(b):
                    dve.wait_ge(s_sf, b + 1)
                    for t in range(T):
                        at = slice(NH2 + HT * t, NH2 + HT * (t + 1))
                        last = nc.vector.tensor_copy(sdh[:, t, at], sd[:, t])
                    last.then_inc(s_sh, 1)
                    dve.wait_ge(s_sh, b + 1)
                    for t in range(T):
                        at = slice(NH2 + HT * t, NH2 + HT * (t + 1))
                        last = nc.vector.tensor_tensor(sdl[:, t, at], sd[:, t],
                                                       sdh[:, t, at].bitcast(F32), ALU.subtract)
                    last.then_inc(s_sl, 1)

                def vk_lo(b):
                    dve.wait_ge(s_p4, b + 1)
                    nc.vector.tensor_tensor(vkl[:].rearrange("p t n -> p (t n)"), ps_p[1][:],
                                            vkh[:].rearrange("p t n -> p (t n)").bitcast(F32),
                                            ALU.subtract).then_inc(s_p5, 1)

                def mt_lo(b, par, bank):
                    dve.wait_ge(s_p7, b * 2 + bank + 1)
                    hi, lo = (v[par][:, 2 * bank:2 * bank + 2, :].rearrange("p t n -> p (t n)")
                              for v in (mth, mtl))
                    nc.vector.tensor_tensor(lo, ps_p[bank][:], hi.bitcast(F32), ALU.subtract).then_inc(s_p8, 1)

                def body(b, last, par):
                    for J in range(PAIRS):
                        norms(b, 2 * J + 1)
                        if J + 1 < PAIRS or not last:
                            invert(b, J + 1)
                            if J == PAIRS - 2 and not last:
                                prep_sden(b + 1)
                            norms(b, 2 * J + 2)
                        if not last:
                            if J == 0:
                                prep_diag(b + 1)
                            if J == 1:
                                vk_lo(b + 1)
                            if J == 2:
                                for bank in range(2):
                                    mt_lo(b + 1, 1 - par, bank)

                dve.sem_inc(s_rl, 1)
                dve.sem_inc(s_n, 2)
                nc.vector.memset(qn[0][:], 0.0).then_inc(s_z, 1)
                dve.wait_ge(s_z, 1)
                zeros = qn[0][:, 0:3 * NH2].rearrange("p (t n) -> p t n", t=1).broadcast_to([P, T, 3 * NH2])
                for v in (sdh, sdl):
                    nc.vector.tensor_copy(v[:], zeros).then_inc(s_z, 1)
                dve.wait_ge(s_c, 3)
                nc.vector.tensor_copy(spread[:].rearrange("p t n -> p (t n)"),
                                      spread_f[:].rearrange("p t n -> p (t n)")).then_inc(s_z, 1)
                dve.wait_ge(s_z, 4)
                prep_diag(0)
                prep_sden(0)
                vk_lo(0)
                for bank in range(2):
                    mt_lo(0, 0, bank)
                invert(0, 0)
                norms(0, 0)
                by_batch(dve, body)

            @block.tensor
            def _(pe):
                def den_tile(b, J, t):
                    pe.wait_ge(s_ql, (b * CHUNKS + 2 * J + 1) * T + t + 1)
                    for k in range(2):
                        cols = slice(NH2, 3 * NH2) if k == 0 else slice(0, 2 * NH2)
                        ws = (sdh[:, t, cols], sdl[:, t, cols])
                        for i, (w, mv) in enumerate(split_passes(ws[0], ws[1], qh[k][:, t], ql[k][:, t])):
                            last = nc.tensor.matmul(ps_den[:], w, mv, start=(t == 0 and k == 0 and i == 0),
                                                    stop=(t == T - 1 and k == 1 and i == 2))
                    if t == T - 1:
                        last.then_inc(s_den, 1)

                def den_start(b, J):
                    if J == 0:
                        pe.wait_ge(s_sl, b + 1)

                def spread_rec(b, c, t):
                    if t == 0:
                        pe.wait_ge(s_rl, b * CHUNKS + c + 2)
                    pe.wait_ge(s_n, (b * CHUNKS + c) * T + t + 1)
                    nc.tensor.matmul(ps_r[t % 2][:], spread[:, t], rec[c % 2][:], start=True,
                                     stop=True).then_inc(s_r, 1)

                def project(b, c, par, between):
                    if c == 0:
                        pe.wait_ge(s_p8, b * 2 + 2)
                    for kt in range(KT):
                        pe.wait_ge(s_bn, (b * CHUNKS + c) * KT + kt + 1)
                        for t in range(T):
                            if kt == 0:
                                pe.wait_ge(s_nl, (b * CHUNKS + c) * T + t + 1)
                            ws = [v[par][:, t, kt * P:(kt + 1) * P] for v in (mth, mtl)]
                            for i, (w, mv) in enumerate(split_passes(ws[0], ws[1], nh[c % 2][:, t],
                                                                     nl[c % 2][:, t])):
                                last = nc.tensor.matmul(ps_y[kt][:], w, mv, start=(t == 0 and i == 0),
                                                        stop=(t == T - 1 and i == 2))
                            if t == T - 1:
                                last.then_inc(s_y, 1)
                            if t % 2:
                                between(kt * 2 + t // 2)

                def prep_sums(b):
                    for t in range(KT):
                        n = HT * (DIM + 1)
                        src = keep["vk_b"][:, bass.ds(b, 1), t * HT:(t + 1) * HT, :]
                        last = nc.tensor.matmul(ps_p[0][:, t * n:(t + 1) * n], keep["dimsel"][:],
                                                src.rearrange("p a h e -> p (a h e)"), start=True, stop=True)
                    last.then_inc(s_p1, 1)

                def prep_transposes(b):
                    pe.wait_ge(s_p2, b + 1)
                    for t in range(T):
                        last = nc.tensor.transpose(ps_p[1][:, t * P:(t + 1) * P], vkd[:, t], keep["ident"][:])
                    last.then_inc(s_p3, 1)

                def prep_products(b):
                    pe.wait_ge(s_p5, b + 1)
                    for bank in range(2):
                        for k in range(2):
                            t = 2 * bank + k
                            for i, (w, mv) in enumerate(split_passes(vkh[:, t], vkl[:, t], keep["wp_hi"][:, t],
                                                                     keep["wp_lo"][:, t])):
                                last = nc.tensor.matmul(ps_p[bank][:, k * C:(k + 1) * C], w, mv,
                                                        start=(i == 0), stop=(i == 2))
                        last.then_inc(s_p6, 1)

                def body(b, last, par):
                    for J in range(PAIRS):
                        ahead = J + 1 < PAIRS or not last
                        if J + 1 < PAIRS:
                            nb, nJ = b, J + 1
                        else:
                            nb, nJ = b + 1, 0
                        if ahead:
                            den_start(nb, nJ)
                            pe.wait_ge(s_de, b * PAIRS + J + 1)
                        for t in range(T):
                            if ahead:
                                den_tile(nb, nJ, t)
                            spread_rec(b, 2 * J + 1, t)
                        project(b, 2 * J, par, lambda n: None)
                        if not last:
                            if J == 0:
                                pe.wait_ge(s_p8, b * 2 + 2)
                                prep_sums(b + 1)
                            if J == 1:
                                prep_transposes(b + 1)
                            if J == 2:
                                prep_products(b + 1)
                        project(b, 2 * J + 1, par,
                                (lambda n: spread_rec(b, 2 * J + 2, n)) if ahead else (lambda n: None))

                pe.sem_inc(s_den, 1)
                pe.sem_inc(s_r, 1)
                pe.sem_inc(s_y, 4)
                pe.wait_ge(s_z, 4)
                prep_sums(0)
                prep_transposes(0)
                prep_products(0)
                den_start(0, 0)
                for t in range(T):
                    den_tile(0, 0, t)
                for t in range(T):
                    spread_rec(0, 0, t)
                by_batch(pe, body)


def bass_conv_linear_attention_kernel(nc, x, w_qkv, w_dw, w_pw, w_proj, bn_gamma, bn_beta, bn_mean, bn_var, out):
    n_batch = x.shape[0]
    grid_d = nc.dram_tensor("grid", [n_batch, PARTS * C, STG], F32, kind="Internal").ap()
    q_d = nc.dram_tensor("relu_q", [n_batch, 2 * C, NPIX], F32, kind="Internal").ap()
    kern_d = nc.dram_tensor("kernels", [PARTS * HEADS, DIM, KROW], F32, kind="Internal").ap()
    x_d = x.rearrange("b c h w -> b c (h w)")
    out_d = out.rearrange("b c h w -> b c (h w)")
    with ExitStack() as ctx:
        keep = kept(nc, ctx, n_batch)
        with ExitStack() as own:
            m = Mem(nc, own)
            keep["wq_hi"] = m.sb("wq_hi", [P, KT, PARTS * C], F32R)
            keep["wq_lo"] = m.sb("wq_lo", [P, KT, PARTS * C], F32R)
            phase0_weights(nc, keep, w_qkv, w_dw, w_pw, w_proj, bn_gamma, bn_beta, bn_mean, bn_var, kern_d)
            phase1_qkv(nc, keep, x_d, grid_d, q_d, n_batch)
        keep["vk_b"] = Mem(nc, ctx).sb("vk_b", [P, n_batch, HEADS, DIM + 1])
        phase2_agg(nc, keep, kern_d, grid_d, q_d, n_batch, HEADS)
        phase3_out(nc, keep, x_d, q_d, out_d, n_batch)


_INS = ["x", "L0_conv_w_qkv", "L0_conv_w_dw", "L0_conv_w_pw", "L0_conv_w_proj", "L0_conv_bn_gamma",
        "L0_conv_bn_beta", "L0_conv_bn_mean", "L0_conv_bn_var"]


def kernel(**inputs):
    import numpy as _np
    import concourse.bacc as _bacc
    from concourse import mybir as _mybir
    from concourse.bass_utils import run_bass_kernel_spmd as _run

    nc = _bacc.Bacc("TRN2", target_bir_lowering=False, num_devices=1)
    arrays, args = {}, []
    for name in _INS:
        a = _np.ascontiguousarray(inputs[name])
        arrays[f"in_{name}"] = a
        args.append(nc.dram_tensor(f"in_{name}", a.shape, _mybir.dt.from_np(a.dtype), kind="ExternalInput").ap())
    args.append(nc.dram_tensor("out_0", inputs["x"].shape, _mybir.dt.float32, kind="ExternalOutput").ap())
    bass_conv_linear_attention_kernel(nc, *args)
    r = _run(nc, [arrays], core_ids=[0])
    return r.results[0]["out_0"]
```

```python
from contextlib import ExitStack

import concourse.bass as bass
from concourse import mybir

F32 = mybir.dt.float32
F32R = mybir.dt.float32r
ALU = mybir.AluOpType
ACT = mybir.ActivationFunctionType
AX_X = mybir.AxisListType.X

P = 128
C = 256
H = W = 64
NPIX = H * W
DIM = 8
HEADS = C // DIM
KT = C // P
PATCH = 4
NPL = PATCH * PATCH
NB = H // PATCH
PLANE = NB * NB
GS = NB + 1
GRID = GS * GS
STG = NPL * GRID
TAPS = 5
PADK = 11
KROW = DIM * PADK * PADK
RWIN = KROW - 3 * PADK - 3
BANK = 512
HT = P // DIM
PARTS = 3
EPS = 1e-15
BN_EPS = 1e-5


class Mem:

    def __init__(self, nc, ctx):
        self.nc, self.ctx = nc, ctx

    def sb(self, name, shape, dt=F32):
        return self.ctx.enter_context(self.nc.sbuf_tensor(name, shape, dt))

    def ps(self, name, shape=(P, BANK)):
        return self.ctx.enter_context(self.nc.psum_tensor(name, list(shape), F32))

    def sem(self, name):
        return self.ctx.enter_context(self.nc.semaphore(name))


def split_passes(hi_w, lo_w, hi_x, lo_x):
    return ((hi_w, hi_x), (lo_w, hi_x), (hi_w, lo_x))


def load_x(nc, keep, sp, x_d, b):
    for kt in range(KT):
        sp.dma_start(keep["xraw"][:, kt, :], x_d[b, kt * P:(kt + 1) * P, :]).then_inc(keep["x_loaded"], 16)


def phase0_weights(nc, keep, x_d, w_qkv, w_dw, w_pw, w_proj, bn_gamma, bn_beta, bn_mean, bn_var, kern_d):
    G = PARTS * HEADS
    with ExitStack() as ctx:
        m = Mem(nc, ctx)
        wq_nat = m.sb("wq_nat", [P, PARTS * KT, C])
        wp_nat = m.sb("wp_nat", [P, KT, 2 * C])
        dw_sb = m.sb("dw_sb", [G, DIM, TAPS * TAPS])
        pw_sb = m.sb("pw_sb", [G, DIM, DIM])
        kern = m.sb("kern_sb", [G, DIM, DIM, PADK, PADK])
        bn_sb = m.sb("bn_sb", [P, 4, KT])
        bn_t = m.sb("bn_t", [P, 2, KT])
        bn_r = m.sb("bn_r", [P, KT])
        ps = [m.ps(f"ps0_{i}") for i in range(4)]
        s_w = m.sem("p0_w_loaded")
        s_c = m.sem("p0_conv_loaded")
        s_b = m.sem("p0_bn_loaded")
        s_mask = m.sem("p0_masks")
        s_tp = m.sem("p0_transposed")
        s_hi = m.sem("p0_hi_made")
        s_lo = m.sem("p0_lo_made")
        s_v = m.sem("p0_vector_step")
        s_bn = m.sem("p0_bn_root")
        s_kern = m.sem("p0_kernels_made")
        s_st = m.sem("p0_kernels_stored")
        jobs = [("q", o, kt) for kt in range(KT) for o in range(PARTS * KT)] \
            + [("p", t, ot) for ot in range(KT) for t in range(2 * KT)]

        def source(job):
            kind, a, b = job
            return wq_nat[:, a, b * P:(b + 1) * P] if kind == "q" else wp_nat[:, b, a * P:(a + 1) * P]

        def target(job, which):
            kind, a, b = job
            if kind == "q":
                return keep[f"wq_{which}"][:, b, a * P:(a + 1) * P]
            return keep[f"wp_{which}"][:, a, b * P:(b + 1) * P]

        with nc.Block() as block:
            @block.sync
            def _(sp):
                w_v = w_qkv.rearrange("(h j i) c -> j h i c", j=PARTS, i=DIM)
                for j in range(PARTS):
                    for half in range(KT):
                        sp.dma_start(wq_nat[:, j * KT + half, :],
                                     w_v[j, half * HT:(half + 1) * HT]).then_inc(s_w, 16)
                sp.dma_start(wp_nat[:], w_proj.rearrange("(t p) c -> p t c", p=P)).then_inc(s_w, 16)
                load_x(nc, keep, sp, x_d, 0)
                sp.wait_ge(s_kern, 1)
                sp.dma_start(kern_d.rearrange("g i k -> g (i k)"),
                             kern[:].rearrange("g i o a b -> g (i o a b)")).then_inc(s_st, 16)
                sp.wait_ge(s_st, 16)

            @block.scalar
            def _(act):
                act.dma_start(dw_sb[:], w_dw.rearrange("(g i) a b c -> g i (a b c)", i=DIM)).then_inc(s_c, 16)
                act.dma_start(pw_sb[:], w_pw.rearrange("(g o) i -> g o i", o=DIM)).then_inc(s_c, 16)
                for n, a in enumerate((bn_gamma, bn_beta, bn_mean, bn_var)):
                    with nc.allow_non_contiguous_dma(reason="256 values"):
                        act.dma_start(bn_sb[:, n, :], a.rearrange("(t p) -> p t", p=P)).then_inc(s_b, 16)
                act.wait_ge(s_v, 3)
                nc.scalar.activation(bn_t[:, 1, :], bn_t[:, 0, :], ACT.Sqrt).then_inc(s_bn, 1)
                for n, job in enumerate(jobs):
                    act.wait_ge(s_tp, n + 1)
                    nc.scalar.activation(target(job, "hi"), ps[n % 4][:, 0:P], ACT.Copy).then_inc(s_hi, 1)

            @block.vector
            def _(dve):
                nc.vector.memset(kern[:].rearrange("g i o a b -> g (i o a b)"), 0.0).then_inc(s_v, 1)
                dve.wait_ge(s_v, 1)
                dve.wait_ge(s_c, 32)
                for ty in range(TAPS):
                    for tx in range(TAPS):
                        dw = dw_sb[:, :, ty * TAPS + tx:ty * TAPS + tx + 1].broadcast_to([G, DIM, DIM])
                        last = nc.vector.tensor_tensor(kern[:, :, :, ty + 3, tx + 3],
                                                       pw_sb[:].rearrange("g o i -> g i o"), dw, ALU.mult)
                last.then_inc(s_kern, 1)
                nc.vector.memset(keep["eps"][:], EPS).then_inc(s_v, 1)
                dve.wait_ge(s_b, 64)
                nc.vector.tensor_scalar_add(bn_t[:, 0, :], bn_sb[:, 3, :], BN_EPS).then_inc(s_v, 1)
                dve.wait_ge(s_bn, 1)
                nc.vector.reciprocal(bn_r[:], bn_t[:, 1, :]).then_inc(s_v, 1)
                dve.wait_ge(s_v, 4)
                nc.vector.tensor_tensor(bn_r[:], bn_r[:], bn_t[:, 0, :], ALU.mult).then_inc(s_v, 1)
                dve.wait_ge(s_v, 5)
                nc.vector.tensor_tensor(bn_r[:], bn_r[:], bn_t[:, 1, :], ALU.add).then_inc(s_v, 1)
                dve.wait_ge(s_v, 6)
                nc.vector.tensor_scalar_mul(bn_r[:], bn_r[:], 0.5).then_inc(s_v, 1)
                dve.wait_ge(s_v, 7)
                nc.vector.reciprocal(bn_t[:, 0, :], bn_r[:]).then_inc(s_v, 1)
                dve.wait_ge(s_v, 8)
                nc.vector.tensor_tensor(keep["bn_scale"][:], bn_sb[:, 0, :], bn_t[:, 0, :],
                                        ALU.mult).then_inc(s_v, 1)
                dve.wait_ge(s_v, 9)
                nc.vector.tensor_tensor(bn_t[:, 1, :], bn_sb[:, 2, :], keep["bn_scale"][:],
                                        ALU.mult).then_inc(s_v, 1)
                dve.wait_ge(s_v, 10)
                nc.vector.tensor_tensor(keep["bn_bias"][:], bn_sb[:, 1, :], bn_t[:, 1, :], ALU.subtract)
                for n, job in enumerate(jobs):
                    dve.wait_ge(s_hi, n + 1)
                    nc.vector.tensor_tensor(target(job, "lo"), ps[n % 4][:, 0:P],
                                            target(job, "hi").bitcast(F32), ALU.subtract).then_inc(s_lo, 1)

            @block.gpsimd
            def _(pool):
                for n, (t, value) in enumerate((("ident", 0.0), ("headmask", 1.0), ("planemask", 0.0),
                                                ("dimsel", 0.0))):
                    nc.gpsimd.memset(keep[t][:], value).then_inc(s_mask, 1)
                pool.wait_ge(s_mask, 4)
                sel = nc.gpsimd.affine_select
                sel(out=keep["ident"][:], in_=keep["ident"][:], compare_op=ALU.not_equal, fill=1.0, base=0,
                    pattern=[[-1, P]], channel_multiplier=1).then_inc(s_mask, 1)
                sel(out=keep["headmask"][:], in_=keep["headmask"][:], compare_op=ALU.is_ge, fill=0.0, base=0,
                    pattern=[[-DIM, HT]], channel_multiplier=1).then_inc(s_mask, 1)
                for k in range(DIM):
                    pool.wait_ge(s_mask, 6 + k)
                    sel(out=keep["planemask"][:], in_=keep["planemask"][:], compare_op=ALU.not_equal,
                        fill=1.0, base=-NPL * k, pattern=[[-1, NPL]], channel_multiplier=1).then_inc(s_mask, 1)
                pool.wait_ge(s_mask, 14)
                sel(out=keep["headmask"][:], in_=keep["headmask"][:], compare_op=ALU.is_ge, fill=0.0,
                    base=DIM - 1, pattern=[[DIM, HT]], channel_multiplier=-1).then_inc(s_mask, 1)
                for r in range(NPL):
                    pool.wait_ge(s_mask, 15 + r)
                    v = keep["dimsel"][:].rearrange("p (h d) -> p h d", d=DIM)
                    sel(out=v, in_=v, compare_op=ALU.not_equal, fill=1.0, base=-r,
                        pattern=[[0, HT], [-NPL, DIM]], channel_multiplier=1).then_inc(s_mask, 1)
                pool.wait_ge(s_mask, 15 + NPL)

            @block.tensor
            def _(pe):
                pe.wait_ge(s_w, 16 * (PARTS * KT + 1))
                pe.wait_ge(s_mask, 5)
                for n, job in enumerate(jobs):
                    if n >= 4:
                        pe.wait_ge(s_lo, n - 3)
                    nc.tensor.transpose(ps[n % 4][:, 0:P], source(job), keep["ident"][:]).then_inc(s_tp, 1)


def phase1_qkv(nc, keep, x_d, grid_d, q_d, n_batch):
    TILES = PARTS * KT
    NBK = NPIX // BANK
    NT = TILES * NBK
    UNITS = STG // (2 * P)
    assert (KT * UNITS) % 4 == 0 and STG - UNITS * 2 * P <= GS
    with ExitStack() as ctx:
        m = Mem(nc, ctx)
        xraw = keep["xraw"]
        xh = m.sb("xh", [P, KT, NPL, PLANE], F32R)
        xl = m.sb("xl", [P, KT, NPL, PLANE], F32R)
        stage = [m.sb(f"stage_{'qkv'[j]}", [P, NPL, GS, GS]) for j in range(PARTS)]
        qbuf = m.sb("qbuf", [P, NPL, PLANE])
        kh = m.sb("kh", [P, 4, 2, P], F32R)
        kl = m.sb("kl", [P, 4, 2, P], F32R)
        vt = m.sb("vt", [P, 4, 2, 2 * P + 2], F32R)
        vk_m = m.sb("vk_m", [P, DIM, 2 * HT])
        ps_qkv = [m.ps(f"ps_qkv{i}") for i in range(2)]
        ps_t = [m.ps(f"ps_t{i}") for i in range(4)]
        ps_vk = [m.ps(f"ps_vk{i}") for i in range(KT)]
        s_x = keep["x_loaded"]
        s_zero = m.sem("ones_and_borders_set")
        s_xh = m.sem("xh_made")
        s_xl = m.sem("xl_made")
        s_mm = m.sem("qkv_bank_made")
        s_ev = [m.sem("even_bank_staged"), m.sem("odd_bank_staged")]
        s_q = m.sem("relu_q_made")
        s_tp = m.sem("unit_transposed")
        s_th = m.sem("unit_hi_made")
        s_tl = m.sem("unit_lo_made")
        s_vk = m.sem("unit_vk_made")
        s_acc = m.sem("vk_read")
        s_m = m.sem("vk_masked")
        s_st = [m.sem(f"stage_{'qkv'[j]}_stored") for j in range(PARTS)]
        s_qst = m.sem("relu_q_stored")
        LOADS = 16 * KT
        AHEAD = 2
        LAG = 4

        def x_view(kt, yo):
            v = xraw[:, kt, :].rearrange("p (by yo bx xo) -> p yo xo by bx", yo=PATCH, by=NB, bx=NB)
            return v[:, yo]

        def x_target(buf, kt, yo):
            return buf[:, kt, yo * PATCH:(yo + 1) * PATCH, :].rearrange("p a (b c) -> p a b c", c=NB)

        def shifted(j, bank):
            yo, xo = bank // 2, 2 * (bank % 2)
            yi, xi = (yo + 2) % PATCH, (xo + 2) % PATCH
            y0, x0 = int(yo >= 2), int(xo >= 2)
            return stage[j][:, yi * PATCH + xi:yi * PATCH + xi + 2, y0:y0 + NB, x0:x0 + NB]

        def planes(ap):
            return ap.rearrange("p (a b c) -> p a b c", b=NB, c=NB)

        def staged_wait(eng, b, n):
            eng.wait_ge(s_ev[n % 2], b * (NT // 2) + n // 2 + 2)

        def unit_tile(j, u, t):
            at = (2 * u + t) * P
            return stage[j][:].rearrange("p a b c -> p (a b c)")[:, at:at + P]

        def slot(half, u):
            return (half * UNITS + u) % 4

        def transposed(n):
            for at in (0, 2 * P):
                yield ps_t[n][:, at:at + 2 * P].rearrange("p (a b) -> p a b", a=2)

        with nc.Block() as block:
            @block.sync
            def _(sp):
                def stores(b):
                    for t in range(TILES):
                        half, j = t // PARTS, t % PARTS
                        staged_wait(sp, b, t * NBK + NBK - 2)
                        staged_wait(sp, b, t * NBK + NBK - 1)
                        row = (j * KT + half) * P
                        sp.dma_start(grid_d[b, row:row + P, :],
                                     stage[j][:].rearrange("p a b c -> p (a b c)")).then_inc(s_st[j], 16)
                        if j == 0:
                            sp.wait_ge(s_q, b * (KT * NBK) + (half + 2) * NBK)
                            sp.dma_start(q_d[b, half * P:(half + 1) * P, :],
                                         qbuf[:].rearrange("p a b -> p (a b)")).then_inc(s_qst, 16)

                for j in range(PARTS):
                    sp.sem_inc(s_st[j], 16)
                sp.sem_inc(s_qst, 16)
                sp.wait_ge(s_zero, PARTS + 1)
                with sp.Fori(0, n_batch - 1) as b:
                    sp.wait_ge(s_xh, b * (KT * PATCH) + KT * PATCH)
                    sp.wait_ge(s_xl, b * (KT * PATCH) + KT * PATCH)
                    load_x(nc, keep, sp, x_d, b + 1)
                    stores(b)
                stores(n_batch - 1)
                for j in range(PARTS):
                    sp.wait_ge(s_st[j], 16 * (KT * n_batch + 1))
                sp.wait_ge(s_qst, 16 * (KT * n_batch + 1))

            @block.scalar
            def _(act):
                def split_hi(b, yo):
                    act.wait_ge(s_x, b * LOADS + LOADS)
                    for kt in range(KT):
                        nc.scalar.activation(x_target(xh, kt, yo), x_view(kt, yo), ACT.Copy).then_inc(s_xh, 1)

                def body(b, last):
                    for t in range(TILES):
                        half, j = t // PARTS, t % PARTS
                        act.wait_ge(s_st[j], (b * KT + half) * 16 + 16)
                        if j > 0:
                            act.wait_ge(s_tl, (b * KT + half) * UNITS + 4)
                        else:
                            act.wait_ge(s_q, (b * KT + half) * NBK + NBK)
                        for bank in range(0, NBK, 2):
                            n = t * NBK + bank
                            act.wait_ge(s_mm, b * NT + n + 1)
                            nc.scalar.activation(shifted(j, bank), planes(ps_qkv[0][:]),
                                                 ACT.Copy).then_inc(s_ev[0], 1)
                            if t == TILES - 1 and not last:
                                yo = bank // 2
                                act.wait_ge(s_mm, b * NT + n + 2)
                                split_hi(b + 1, yo)
                        if j == PARTS - 1:
                            chunk_hi(b, half)

                def chunk_hi(b, half):
                    for u in range(UNITS):
                        k = (b * KT + half) * UNITS + u
                        act.wait_ge(s_tp, k + 1)
                        act.wait_ge(s_vk, k + 1)
                        n = slot(half, u)
                        k_t, v_t = transposed(n)
                        nc.scalar.activation(kh[:, n], k_t, ACT.Relu)
                        nc.scalar.activation(vt[:, n, :, P:2 * P], v_t, ACT.Copy).then_inc(s_th, 1)

                act.sem_inc(s_ev[0], 1)
                for yo in range(PATCH):
                    split_hi(0, yo)
                with act.Fori(0, n_batch - 1) as b:
                    body(b, False)
                body(n_batch - 1, True)

            @block.gpsimd
            def _(pool):
                def split_lo(b, yo):
                    pool.wait_ge(s_xh, b * (KT * PATCH) + KT * (yo + 1))
                    for kt in range(KT):
                        nc.gpsimd.tensor_tensor(x_target(xl, kt, yo), x_view(kt, yo),
                                                x_target(xh, kt, yo).bitcast(F32), ALU.subtract).then_inc(s_xl, 1)

                nc.gpsimd.memset(vt[:, :, :, 2 * P:].bitcast(F32), 1.0).then_inc(s_zero, 1)
                for j in range(PARTS):
                    nc.gpsimd.memset(stage[j][:].rearrange("p a b c -> p (a b c)"), 0.0).then_inc(s_zero, 1)
                with pool.Fori(0, n_batch - 1) as b:
                    for yo in range(PATCH):
                        split_lo(b + 1, yo)

            @block.vector
            def _(dve):
                def stage_bank(b, t, bank):
                    half, j = t // PARTS, t % PARTS
                    n = t * NBK + bank
                    if bank == 1:
                        dve.wait_ge(s_st[j], (b * KT + half) * 16 + 16)
                        if j == 0:
                            dve.wait_ge(s_qst, (b * KT + half) * 16 + 16)
                    dve.wait_ge(s_mm, b * NT + n + 1)
                    nc.vector.tensor_copy(shifted(j, bank), planes(ps_qkv[1][:])).then_inc(s_ev[1], 1)
                    if j == 0:
                        staged_wait(dve, b, n - 1)
                        staged_wait(dve, b, n)
                        for k in (bank - 1, bank):
                            nc.vector.tensor_scalar_max(
                                planes(qbuf[:, 2 * k:2 * k + 2, :].rearrange("p a b -> p (a b)")),
                                shifted(j, k), 0.0).then_inc(s_q, 1)

                def body(b, last):
                    for t in range(TILES):
                        half, j = t // PARTS, t % PARTS
                        for bank in range(1, NBK, 2):
                            if j > 0 or bank > 1:
                                stage_bank(b, t, bank)
                        if j == PARTS - 1:
                            chunk_lo(b, half)
                            if half < KT - 1:
                                stage_bank(b, t + 1, 1)
                            elif not last:
                                stage_bank(b + 1, 0, 1)
                            read_vk(b, half)

                def chunk_lo(b, half):
                    for u in range(UNITS):
                        dve.wait_ge(s_th, (b * KT + half) * UNITS + u + 1)
                        n = slot(half, u)
                        k_t, v_t = transposed(n)
                        nc.vector.scalar_tensor_tensor(kl[:, n], k_t, 0.0, kh[:, n].bitcast(F32),
                                                       ALU.max, ALU.subtract)
                        nc.vector.tensor_tensor(vt[:, n, :, 0:P], v_t, vt[:, n, :, P:2 * P].bitcast(F32),
                                                ALU.subtract).then_inc(s_tl, 1)

                def read_vk(b, half):
                    dve.wait_ge(s_vk, (b * KT + half) * UNITS + UNITS + 4)
                    nc.vector.tensor_tensor(
                        vk_m[:].rearrange("p e (l h) -> p l e h", l=2),
                        ps_vk[half][:, 0:2 * P].rearrange("p (l h e) -> p l e h", l=2, e=DIM),
                        keep["headmask"][:].rearrange("p (l e h) -> p l e h", l=1, e=1
                                                      ).broadcast_to([P, 2, DIM, HT]),
                        ALU.mult).then_inc(s_m, 1)
                    nc.vector.tensor_copy(keep["vk_a"][:, b, half, DIM:],
                                          ps_vk[half][:, 2 * P:2 * P + 1]).then_inc(s_acc, 1)
                    dve.wait_ge(s_m, b * KT + half + 1)
                    nc.vector.tensor_reduce(keep["vk_a"][:, b, half, 0:DIM], vk_m[:], AX_X, ALU.add)

                dve.sem_inc(s_ev[1], 1)
                dve.sem_inc(s_q, NBK)
                dve.sem_inc(s_tl, 4)
                dve.sem_inc(s_acc, KT)
                for yo in range(PATCH):
                    dve.wait_ge(s_xh, KT * (yo + 1))
                    for kt in range(KT):
                        nc.vector.tensor_tensor(x_target(xl, kt, yo), x_view(kt, yo),
                                                x_target(xh, kt, yo).bitcast(F32), ALU.subtract).then_inc(s_xl, 1)
                stage_bank(0, 0, 1)
                with dve.Fori(0, n_batch - 1) as b:
                    body(b, False)
                body(n_batch - 1, True)

            @block.tensor
            def _(pe):
                def tile_banks(b, t, banks):
                    pe.wait_ge(s_zero, 2 + t % PARTS)
                    for bank in banks:
                        n = t * NBK + bank
                        if t == 0 and bank % 2 == 0:
                            yo = bank // 2
                            pe.wait_ge(s_xh, b * (KT * PATCH) + KT * (yo + 1))
                            pe.wait_ge(s_xl, b * (KT * PATCH) + KT * (yo + 1))
                        pe.wait_ge(s_ev[n % 2], b * (NT // 2) + n // 2 + 1)
                        col = (t % PARTS) * KT + t // PARTS
                        k = 0
                        for kt in range(KT):
                            ws = [keep[w][:, kt, col * P:(col + 1) * P] for w in ("wq_hi", "wq_lo")]
                            xs = [v[:, kt, 2 * bank:2 * bank + 2, :] for v in (xh, xl)]
                            for w, mv in split_passes(ws[0], ws[1], xs[0], xs[1]):
                                last = nc.tensor.matmul(ps_qkv[n % 2][:], w, mv, start=(k == 0),
                                                        stop=(k == PARTS * KT - 1))
                                k += 1
                        last.then_inc(s_mm, 1)

                def transposes(b, half, u):
                    pe.wait_ge(s_tl, (b * KT + half) * UNITS + u + 1)
                    for j in (1, 2):
                        for t in range(2):
                            c = ((j - 1) * 2 + t) * P
                            last = nc.tensor.transpose(ps_t[slot(half, u)][:, c:c + P], unit_tile(j, u, t),
                                                       keep["ident"][:])
                    last.then_inc(s_tp, 1)

                def vk(b, half, u):
                    if u == 0:
                        pe.wait_ge(s_acc, b * KT + half + 1)
                    pe.wait_ge(s_tl, (b * KT + half) * UNITS + u + 5)
                    for t in range(2):
                        v = vt[:, slot(half, u), t]
                        nc.tensor.matmul(ps_vk[half][:, 0:2 * P + 2], kh[:, slot(half, u), t], v,
                                         start=(u == 0 and t == 0), stop=False)
                        last = nc.tensor.matmul(ps_vk[half][:, P:2 * P + 2], kl[:, slot(half, u), t], v[:, P:],
                                                start=False, stop=(u == UNITS - 1 and t == 1))
                    last.then_inc(s_vk, 1)

                def chunk(b, half, between):
                    between(0)
                    for n in (NBK - 2, NBK - 1):
                        staged_wait(pe, b, (half * PARTS + 2) * NBK + n)
                    for u in range(LAG):
                        transposes(b, half, u)
                    between(1)
                    for u in range(UNITS):
                        vk(b, half, u)
                        if u + LAG < UNITS:
                            transposes(b, half, u + LAG)

                def body(b, last):
                    for half in range(KT):
                        for j in range(PARTS):
                            tile_banks(b, half * PARTS + j, range(AHEAD if j == 0 else 0, NBK))
                        nb, nt = (b, PARTS) if half == 0 else (b + 1, 0)
                        if half == 0 or not last:
                            chunk(b, half, lambda n: tile_banks(nb, nt, (n,)))
                        else:
                            chunk(b, half, lambda n: None)

                pe.sem_inc(s_vk, 4)
                tile_banks(0, 0, range(AHEAD))
                with pe.Fori(0, n_batch - 1) as b:
                    body(b, False)
                body(n_batch - 1, True)


def kept(nc, ctx, n_batch):
    m = Mem(nc, ctx)
    return {
        "wp_hi": m.sb("wp_hi", [P, 2 * KT, C], F32R), "wp_lo": m.sb("wp_lo", [P, 2 * KT, C], F32R),
        "ident": m.sb("ident", [P, P]), "headmask": m.sb("headmask", [P, HT]),
        "planemask": m.sb("planemask", [P, NPL]), "dimsel": m.sb("dimsel", [P, P]),
        "bn_scale": m.sb("bn_scale", [P, KT]), "bn_bias": m.sb("bn_bias", [P, KT]),
        "eps": m.sb("eps", [P, 1]),
        "vk_a": m.sb("vk_a", [P, n_batch, KT, DIM + 1]),
    }


def phase2_agg(nc, keep, kern_d, grid_d, q_d, n_batch, n_heads):
    NPAIR = n_batch // 2
    SLOTS = PARTS * NPAIR
    UNITS = 2 * NPAIR
    CH = 4
    CHUNKS = PARTS * n_batch // CH
    RING = 3
    PART = (1, 2, 0)
    assert n_batch % CH == 0 and SLOTS % RING == 0 and CHUNKS % RING == 0
    with ExitStack() as ctx:
        m = Mem(nc, ctx)
        xin = [m.sb(f"grid_in{i}", [P, CH, GS, GS]) for i in range(RING)]
        gh = [m.sb(f"grid_hi{i}", [P, 2, GS, GS], F32R) for i in range(RING)]
        gl = [m.sb(f"grid_lo{i}", [P, 2, GS, GS], F32R) for i in range(RING)]
        win = [m.sb(f"window{jj}", [P, KROW]) for jj in range(PARTS)]
        bh = [m.sb(f"band_hi{jj}", [P, 4, DIM, PATCH, PATCH], F32R) for jj in range(PARTS)]
        bl = [m.sb(f"band_lo{jj}", [P, 4, DIM, PATCH, PATCH], F32R) for jj in range(PARTS)]
        kvf = [m.sb(f"kv_agg{i}", [P, BANK]) for i in range(3)]
        qf = [m.sb(f"q_agg{i}", [P, 2, PLANE]) for i in range(2)]
        kth = m.sb("kt_hi", [P, NPAIR, 4, P], F32R)
        ktl = m.sb("kt_lo", [P, NPAIR, 4, P], F32R)
        vt = m.sb("vt_lo_hi", [P, 2, 4, 2, P], F32R)
        vk_m = m.sb("vkb_m", [P, 2, 2, DIM, 2 * NPL])
        ps_c = [m.ps(f"ps_conv{i}") for i in range(RING)]
        ps_t = [m.ps(f"ps_tr{i}") for i in range(2)]
        ps_vk = [m.ps(f"ps_vkb{i}") for i in range(2)]
        s_in = [m.sem(f"grid_in{i}_loaded") for i in range(RING)]
        s_gh = m.sem("grid_hi_made")
        s_gl = m.sem("grid_lo_made")
        s_win = [m.sem(f"window{jj}_loaded") for jj in range(PARTS)]
        s_bhi = m.sem("bands_hi_made")
        s_band = m.sem("bands_made")
        s_conv = m.sem("conv_made")
        s_ev = m.sem("conv_read")
        s_tp = m.sem("agg_transposed")
        s_th = m.sem("agg_hi_made")
        s_tl = m.sem("agg_lo_made")
        s_vk = m.sem("vkb_made")
        s_g = m.sem("vkb_read")
        s_ks = m.sem("ksum_made")
        s_qst = [m.sem(f"q_agg{i}_stored") for i in range(2)]

        def load_window(eng, h, jj):
            for i in range(DIM):
                row = kern_d[h * PARTS + PART[jj], i]
                src = bass.AP(tensor=row.tensor, offset=row.offset,
                              ap=[[PADK, PATCH], [1, PATCH], [1, RWIN]])
                eng.dma_start(win[jj][i * NPL:(i + 1) * NPL, 0:RWIN], src).then_inc(s_win[jj], 16)

        def quadrants(jj):
            w = win[jj][:].rearrange("p (o u w) -> p o u w", o=DIM, u=PADK)
            for a in range(2):
                for b in range(2):
                    us = slice(4 * a + 3, 4 * a - 1 if a else None, -1)
                    ws = slice(4 * b + 3, 4 * b - 1 if b else None, -1)
                    yield 2 * a + b, w[:, :, us, ws]

        with nc.Block() as block:
            @block.sync
            def _(sp):
                def load_grid(h, c):
                    jj, part = c * CH // n_batch, c % (n_batch // CH)
                    sp.wait_ge(s_gl, h * SLOTS + 2 * c + 2)
                    row = (h + PART[jj] * HEADS) * DIM
                    src = grid_d[part * CH:(part + 1) * CH, bass.ds(row, DIM), :]
                    sp.dma_start(xin[c % RING][:].rearrange("p b y x -> p b (y x)"),
                                 src.rearrange("b i (k n) -> (i k) b n", n=GRID)).then_inc(s_in[c % RING], 16)

                def body(h, last):
                    for c in range(CHUNKS):
                        load_grid(h, c)
                        for jj in range(PARTS):
                            if c == min((jj + 1) * CHUNKS // PARTS, CHUNKS - 1) and not last:
                                sp.wait_ge(s_band, h * PARTS + jj + 1)
                                load_window(sp, h + 1, jj)

                with sp.Fori(0, n_heads - 1) as h:
                    body(h, False)
                body(n_heads - 1, True)

            @block.gpsimd
            def _(pool):
                def band_lo(h, jj):
                    pool.wait_ge(s_bhi, h * PARTS + jj + 1)
                    for n, taps in quadrants(jj):
                        last = nc.gpsimd.tensor_tensor(bl[jj][:, n], taps, bh[jj][:, n].bitcast(F32),
                                                       ALU.subtract)
                    last.then_inc(s_band, 1)

                def grid_lo(h, s):
                    pool.wait_ge(s_gh, h * SLOTS + s + 1)
                    s = s % SLOTS
                    c, half = s // 2, s % 2
                    nc.gpsimd.tensor_tensor(
                        gl[s % RING][:].rearrange("p b y x -> p (b y x)"),
                        xin[c % RING][:, 2 * half:2 * half + 2].rearrange("p b y x -> p (b y x)"),
                        gh[s % RING][:].rearrange("p b y x -> p (b y x)").bitcast(F32),
                        ALU.subtract).then_inc(s_gl, 1)

                def body(h, last):
                    for s in range(SLOTS):
                        if s + 2 < SLOTS or not last:
                            grid_lo(h, s + 2)
                        if s == 1:
                            band_lo(h, 2)
                        for jj in (0, 1):
                            if s == (jj + 1) * NPAIR and not last:
                                band_lo(h + 1, jj)

                pool.sem_inc(s_gl, 2 * RING)
                band_lo(0, 0)
                grid_lo(0, 0)
                grid_lo(0, 1)
                band_lo(0, 1)
                with pool.Fori(0, n_heads - 1) as h:
                    body(h, False)
                body(n_heads - 1, True)

            @block.vector
            def _(dve):
                def grid_hi(h, s):
                    dve.wait_ge(s_conv, h * SLOTS + s + 1)
                    wrap, s = s // SLOTS, s % SLOTS
                    c, half = s // 2, s % 2
                    dve.wait_ge(s_in[c % RING], (h + wrap) * (16 * CHUNKS // RING) + 16 * (c // RING + 1))
                    nc.vector.tensor_copy(gh[s % RING][:].rearrange("p b y x -> p (b y x)"),
                                          xin[c % RING][:, 2 * half:2 * half + 2].rearrange("p b y x -> p (b y x)")
                                          ).then_inc(s_gh, 1)

                def band_hi(h, jj):
                    dve.wait_ge(s_win[jj], h * (16 * DIM) + 16 * DIM)
                    for n, taps in quadrants(jj):
                        last = nc.vector.tensor_copy(bh[jj][:, n], taps)
                    last.then_inc(s_bhi, 1)

                def unit_lo(h, u):
                    pair = u % NPAIR
                    dve.wait_ge(s_th, h * UNITS + u + 1)
                    src = ps_t[u % 2][:].rearrange("p (a n) -> p a n", n=P)
                    if u < NPAIR:
                        hi, lo = kth[:, pair], ktl[:, pair]
                    else:
                        hi, lo = vt[:, pair % 2, :, 1], vt[:, pair % 2, :, 0]
                    nc.vector.tensor_tensor(lo, src, hi.bitcast(F32), ALU.subtract).then_inc(s_tl, 1)

                def ksum(h, pair):
                    dve.wait_ge(s_ev, h * SLOTS + pair + 4)
                    nc.vector.tensor_reduce(keep["vk_b"][:, 2 * pair:2 * pair + 2, bass.ds(h, 1), DIM],
                                            kvf[pair % 3][:].rearrange("p (b n) -> p b n", b=2),
                                            AX_X, ALU.add).then_inc(s_ks, 1)

                def collect(h, pair):
                    dve.wait_ge(s_vk, h * NPAIR + pair + 1 + NPAIR)
                    v = ps_vk[pair % 2][:].rearrange("p (b l e k) -> p b l e k", b=2, l=2, k=NPL)
                    for b in range(2):
                        last = nc.vector.tensor_tensor(
                            vk_m[:, pair % 2, b].rearrange("p e (l k) -> p l e k", l=2), v[:, b],
                            keep["planemask"][:].rearrange("p (l e k) -> p l e k", l=1, e=1
                                                           ).broadcast_to([P, 2, DIM, NPL]),
                            ALU.mult)
                    last.then_inc(s_g, 1)
                    dve.wait_ge(s_g, h * NPAIR + pair + 3)
                    nc.vector.tensor_reduce(
                        keep["vk_b"][:, 2 * pair:2 * pair + 2, bass.ds(h, 1), 0:DIM],
                        vk_m[:, pair % 2], AX_X, ALU.add)

                def body(h, last):
                    for s in range(SLOTS):
                        if s + 2 < SLOTS or not last:
                            grid_hi(h, s + 2)
                        if s == 1:
                            dve.wait_ge(s_conv, h * SLOTS + 3)
                            band_hi(h, 2)
                        for jj in (0, 1):
                            if s == (jj + 1) * NPAIR and not last:
                                dve.wait_ge(s_conv, h * SLOTS + (jj + 1) * NPAIR + 3)
                                band_hi(h + 1, jj)
                        if s < NPAIR:
                            ksum(h, s)
                        if 2 <= s < UNITS + 2:
                            unit_lo(h, s - 2)
                        if NPAIR + 3 <= s < UNITS + 3:
                            collect(h, s - NPAIR - 3)

                dve.sem_inc(s_tl, 2)
                dve.sem_inc(s_g, 2)
                dve.sem_inc(s_ks, 3)
                band_hi(0, 0)
                grid_hi(0, 0)
                grid_hi(0, 1)
                band_hi(0, 1)
                with dve.Fori(0, n_heads - 1) as h:
                    body(h, False)
                body(n_heads - 1, True)

            @block.scalar
            def _(act):
                def read_conv(h, s):
                    jj, pair = s // NPAIR, s % NPAIR
                    act.wait_ge(s_conv, h * SLOTS + s + 4)
                    if jj < 2:
                        act.wait_ge(s_tp, h * UNITS + max(s, 2))
                        act.wait_ge(s_ks, h * NPAIR + min(max(s + 1, 3), NPAIR + 3))
                        nc.scalar.activation(kvf[s % 3][:], ps_c[s % RING][:],
                                             ACT.Relu if jj == 0 else ACT.Copy).then_inc(s_ev, 1)
                    else:
                        act.wait_ge(s_qst[pair % 2], h * (16 * NPAIR // 2) + 16 * (pair // 2 + 1))
                        nc.scalar.activation(qf[pair % 2][:].rearrange("p b n -> p (b n)"), ps_c[s % RING][:],
                                             ACT.Relu).then_inc(s_ev, 1)

                def store_q(h, pair):
                    act.wait_ge(s_ev, h * SLOTS + 2 * NPAIR + pair + 4)
                    dst = q_d[2 * pair:2 * pair + 2, bass.ds(C + h * DIM, DIM), :]
                    act.dma_start(dst.rearrange("b o (k n) -> (o k) b n", n=PLANE),
                                  qf[pair % 2][:]).then_inc(s_qst[pair % 2], 16)

                def unit_hi(h, u):
                    pair = u % NPAIR
                    act.wait_ge(s_tp, h * UNITS + u + 3)
                    src = ps_t[u % 2][:].rearrange("p (a n) -> p a n", n=P)
                    if u < NPAIR:
                        act.wait_ge(s_vk, h * NPAIR + pair + 1)
                        dst = kth[:, pair]
                    else:
                        act.wait_ge(s_vk, h * NPAIR + pair - 1 + NPAIR)
                        dst = vt[:, pair % 2, :, 1]
                    nc.scalar.activation(dst, src, ACT.Copy).then_inc(s_th, 1)

                def body(h):
                    for s in range(SLOTS):
                        read_conv(h, s)
                        if 2 <= s < UNITS + 2:
                            unit_hi(h, s - 2)
                        if s > 2 * NPAIR:
                            store_q(h, s - 2 * NPAIR - 1)
                    store_q(h, NPAIR - 1)

                act.sem_inc(s_ev, RING)
                for i in range(2):
                    act.sem_inc(s_qst[i], 16)
                for jj in range(PARTS):
                    load_window(act, 0, jj)
                with act.Fori(0, n_heads) as h:
                    body(h)
                for i in range(2):
                    act.wait_ge(s_qst[i], 16 * (n_heads * NPAIR // 2 + 1))

            @block.tensor
            def _(pe):
                def conv(h, s):
                    jj = s // NPAIR
                    if s % NPAIR == 0:
                        pe.wait_ge(s_band, h * PARTS + jj + 1)
                    pe.wait_ge(s_gl, h * SLOTS + s + 1 + 2 * RING)
                    pe.wait_ge(s_ev, h * SLOTS + s + 1)
                    k = 0
                    for a in range(2):
                        for b in range(2):
                            ws = [v[jj][:, 2 * a + b].rearrange("p o y x -> p (o y x)") for v in (bh, bl)]
                            xs = [v[s % RING][:, :, a:a + NB, b:b + NB] for v in (gh, gl)]
                            for w, mv in split_passes(ws[0], ws[1], xs[0], xs[1]):
                                last = nc.tensor.matmul(ps_c[s % RING][:], w, mv, start=(k == 0), stop=(k == 11))
                                k += 1
                    last.then_inc(s_conv, 1)

                def transposes(h, u):
                    pe.wait_ge(s_ev, h * SLOTS + u + 4)
                    pe.wait_ge(s_tl, h * UNITS + u + 1)
                    for t in range(4):
                        last = nc.tensor.transpose(ps_t[u % 2][:, t * P:(t + 1) * P],
                                                   kvf[u % 3][:, t * P:(t + 1) * P], keep["ident"][:])
                    last.then_inc(s_tp, 1)

                def vk(h, pair):
                    pe.wait_ge(s_tl, h * UNITS + NPAIR + pair + 3)
                    pe.wait_ge(s_g, h * NPAIR + pair + 1)
                    for b in range(2):
                        out = ps_vk[pair % 2][:, b * 2 * P:(b + 1) * 2 * P]
                        for t in range(2):
                            v = vt[:, pair % 2, 2 * b + t]
                            nc.tensor.matmul(out, kth[:, pair, 2 * b + t], v.rearrange("p l n -> p (l n)"),
                                             start=(t == 0), stop=False)
                            last = nc.tensor.matmul(out[:, P:], ktl[:, pair, 2 * b + t], v[:, 1],
                                                    start=False, stop=(t == 1))
                    last.then_inc(s_vk, 1)

                pe.sem_inc(s_conv, RING)
                pe.sem_inc(s_tp, 2)
                pe.sem_inc(s_vk, NPAIR)
                with pe.Fori(0, n_heads) as h:
                    for s in range(SLOTS):
                        conv(h, s)
                        if 2 <= s < UNITS + 2:
                            transposes(h, s - 2)
                        if NPAIR + 3 <= s < UNITS + 3:
                            vk(h, s - NPAIR - 3)


def phase3_out(nc, keep, x_d, q_d, out_d, n_batch):
    T = 2 * KT
    CHUNKS = NPIX // BANK
    PAIRS = CHUNKS // 2
    NH2 = 2 * HEADS
    RING = 4
    HALF = CHUNKS // 2
    with ExitStack() as ctx:
        m = Mem(nc, ctx)
        qraw = [m.sb(f"q_raw{i}", [P, T, BANK]) for i in range(RING)]
        qh = [m.sb(f"q_hi{i}", [P, T, BANK], F32R) for i in range(2)]
        ql = [m.sb(f"q_lo{i}", [P, T, BANK], F32R) for i in range(2)]
        qn = [m.sb(f"q_norm{i}", [P, BANK]) for i in range(T)]
        nh = m.sb("q_norm_hi", [P, T, BANK], F32R)
        nl = m.sb("q_norm_lo", [P, T, BANK], F32R)
        xy = [m.sb(f"x_half{i}", [P, KT, NPIX // 2]) for i in range(2)]
        ybn = [m.sb(f"y_bn{i}", [P, KT, BANK]) for i in range(2)]
        mth = [m.sb(f"mt_hi{i}", [P, T, C], F32R) for i in range(2)]
        mtl = [m.sb(f"mt_lo{i}", [P, T, C], F32R) for i in range(2)]
        sdh = m.sb("sden_hi", [P, T, 3 * NH2], F32R)
        sdl = m.sb("sden_lo", [P, T, 3 * NH2], F32R)
        sd = m.sb("sden", [P, T, HT])
        vkd = m.sb("vk_diag", [P, T, P])
        vkh = m.sb("vk_t_hi", [P, T, P], F32R)
        vkl = m.sb("vk_t_lo", [P, T, P], F32R)
        den = m.sb("den", [P, BANK])
        rec = [m.sb(f"rec_hl{i}", [P, BANK], F32R) for i in range(2)]
        spread_f = m.sb("spread_f", [P, T, P])
        spread = m.sb("spread", [P, T, P], F32R)
        ps_den = m.ps("ps_den")
        ps_r = [m.ps(f"ps_rec{i}") for i in range(2)]
        ps_y = [[m.ps(f"ps_y{i}_{kt}") for kt in range(KT)] for i in range(2)]
        ps_p = m.ps("ps_prep")
        s_q = [[m.sem(f"q_raw{i}_tile{t}_loaded") for t in range(T)] for i in range(RING)]
        s_x = [m.sem(f"x_half{i}_loaded") for i in range(2)]
        s_out = [m.sem(f"y_half{i}_stored") for i in range(2)]
        s_c = m.sem("spread_step")
        s_z = m.sem("sden_zeroed")
        s_qh = m.sem("q_hi_made")
        s_ql = m.sem("q_lo_made")
        s_den = m.sem("den_made")
        s_de = m.sem("den_eps_made")
        s_rc = m.sem("den_inverted")
        s_rh = m.sem("rec_hi_made")
        s_rl = m.sem("rec_lo_made")
        s_r = m.sem("rec_spread")
        s_n = m.sem("q_norm_made")
        s_nh = m.sem("q_norm_hi_made")
        s_nl = m.sem("q_norm_lo_made")
        s_y = m.sem("tile_projected")
        s_bn = m.sem("y_bn_made")
        s_add = m.sem("y_added")
        s_p1 = m.sem("prep_sums_made")
        s_p2 = m.sem("prep_diag_made")
        s_sf = m.sem("prep_sden_made")
        s_sh = m.sem("prep_sden_hi_made")
        s_sl = m.sem("prep_sden_lo_made")
        s_p3 = m.sem("prep_transposed")
        s_p4 = m.sem("prep_vk_hi_made")
        s_p5 = m.sem("prep_vk_lo_made")
        s_p6 = m.sem("prep_mt_made")
        s_p7 = m.sem("prep_mt_hi_made")
        s_p8 = m.sem("prep_mt_lo_made")

        def stored_half(buf, half, kt):
            v = buf[kt * P:(kt + 1) * P, :].rearrange("p (by yo x) -> p by yo x", yo=PATCH, x=W)
            return v[:, :, 2 * half:2 * half + 2, :]

        def chunk_of_half(g, kt, c):
            yo, xo = (c // 2) % 2, 2 * (c % 2)
            v = xy[g][:, kt, :].rearrange("p (by yo bx xo) -> p yo xo by bx", yo=2, by=NB, bx=NB)
            return v[:, yo, xo:xo + 2]

        def heads_mask(n):
            return keep["headmask"][:].rearrange("p (h a) -> p h a", a=1).broadcast_to([P, HT, n])

        def by_batch(eng, body):
            with eng.Fori(0, n_batch // 2 - 1) as i:
                body(i * 2, False, 0)
                body(i * 2 + 1, False, 1)
            body(n_batch - 2, False, 0)
            body(n_batch - 1, True, 1)

        with nc.Block() as block:
            @block.sync
            def _(sp):
                def load_tile(b, c, t):
                    sp.dma_start(qraw[c % RING][:, t], q_d[b, t * P:(t + 1) * P, c * BANK:(c + 1) * BANK]
                                 ).then_inc(s_q[c % RING][t], 16)

                def load_q(b, c):
                    for t in range(T):
                        sp.wait_ge(s_n, (b * CHUNKS + c - RING) * T + t + 3)
                        load_tile(b, c, t)

                def load_x(b, half):
                    sp.wait_ge(s_out[half], b * (16 * KT) + 16 * KT)
                    for kt in range(KT):
                        sp.dma_start(xy[half][:, kt, :].rearrange("p (by yo x) -> p by yo x", by=NB, yo=2),
                                     stored_half(x_d[b], half, kt)).then_inc(s_x[half], 16)

                def load_pair(b, J):
                    for c in (2 * J + RING, 2 * J + RING + 1):
                        if c < CHUNKS:
                            load_q(b, c)
                        else:
                            load_q(b + 1, c - CHUNKS)

                def store(b, half):
                    sp.wait_ge(s_add, (b * CHUNKS + (half + 1) * HALF) * KT + 2 * KT)
                    for kt in reversed(range(KT)):
                        sp.dma_start(stored_half(out_d[b], half, kt),
                                     xy[half][:, kt, :].rearrange("p (by yo x) -> p by yo x", by=NB, yo=2)
                                     ).then_inc(s_out[half], 16)

                def body(b, last, par):
                    for J in range(1, PAIRS):
                        if 2 * J + RING < CHUNKS or not last:
                            load_pair(b, J)
                        if J == 1:
                            load_x(b, 1)
                        if J == PAIRS // 2:
                            store(b, 0)
                        if J == PAIRS - 1 and not last:
                            load_x(b + 1, 0)
                    if not last:
                        load_pair(b + 1, 0)
                    store(b, 1)

                for half in range(2):
                    sp.sem_inc(s_out[half], 16 * KT)
                for c in range(RING):
                    for t in range(T):
                        load_tile(0, c, t)
                load_x(0, 0)
                load_pair(0, 0)
                by_batch(sp, body)
                for half in range(2):
                    sp.wait_ge(s_out[half], 16 * KT * (n_batch + 1))

            def raw_loaded(eng, b, c, t):
                eng.wait_ge(s_q[c % RING][t], b * (16 * CHUNKS // RING) + 16 * (c // RING + 1))

            @block.gpsimd
            def _(pool):
                def q_lo(b, c):
                    for t in range(T):
                        pool.wait_ge(s_qh, (b * CHUNKS + c) * T + t + 1)
                        nc.gpsimd.tensor_tensor(ql[c % 2][:, t], qraw[c % RING][:, t],
                                                qh[c % 2][:, t].bitcast(F32), ALU.subtract).then_inc(s_ql, 1)

                def add_x(b, c):
                    for kt in range(KT):
                        half = c // HALF
                        pool.wait_ge(s_x[half], b * (16 * KT) + 16 * KT)
                        pool.wait_ge(s_bn, (b * CHUNKS + c) * KT + kt + 2 * KT + 1)
                        v = chunk_of_half(half, kt, c)
                        nc.gpsimd.tensor_tensor(v, ybn[c % 2][:, kt].rearrange("p (a b c) -> p a b c", a=2, b=NB),
                                                v, ALU.add).then_inc(s_add, 1)

                def body(b, last, par):
                    for J in range(PAIRS):
                        for c in (2 * J + RING, 2 * J + RING + 1):
                            if c < CHUNKS or not last:
                                q_lo(b, c)
                        for c in (2 * J, 2 * J + 1):
                            add_x(b, c)

                pool.sem_inc(s_add, 2 * KT)
                nc.gpsimd.memset(spread_f[:], 0.0).then_inc(s_c, 1)
                for s in range(2):
                    pool.wait_ge(s_c, s + 1)
                    for t in range(T):
                        v = spread_f[:, t].rearrange("p (h e) -> p h e", e=DIM)
                        last = nc.gpsimd.affine_select(
                            out=v, in_=v, compare_op=ALU.not_equal, fill=1.0, base=-NH2 * s - HT * t,
                            pattern=[[-1, HT], [0, DIM]], channel_multiplier=1)
                    last.then_inc(s_c, 1)
                for c in range(4):
                    q_lo(0, c)
                by_batch(pool, body)

            @block.scalar
            def _(act):
                def q_hi(b, c, t):
                    act.wait_ge(s_den, b * PAIRS + c // 2 + 1)
                    raw_loaded(act, b, c, t)
                    nc.scalar.activation(qh[c % 2][:, t], qraw[c % RING][:, t], ACT.Copy).then_inc(s_qh, 1)

                def den_eps(b, J):
                    act.wait_ge(s_den, b * PAIRS + J + 2)
                    act.wait_ge(s_rl, (b * PAIRS + J) * 2 + 1)
                    nc.scalar.activation(den[:], ps_den[:], ACT.Identity, bias=keep["eps"][:]).then_inc(s_de, 1)

                def rec_hi(b, J):
                    act.wait_ge(s_rc, b * PAIRS + J + 1)
                    act.wait_ge(s_r, (b * PAIRS + J) * (2 * T) + 1)
                    for k in range(2):
                        at = slice(k * NH2, (k + 1) * NH2)
                        nc.scalar.activation(rec[k][at, :], den[at, :], ACT.Copy).then_inc(s_rh, 1)

                def norm_hi(b, c, t):
                    act.wait_ge(s_y, (b * CHUNKS + c) * T + t + 1)
                    act.wait_ge(s_n, (b * CHUNKS + c) * T + t + 3)
                    nc.scalar.activation(nh[:, t], qn[t][:], ACT.Copy).then_inc(s_nh, 1)

                def bn(b, c):
                    act.wait_ge(s_y, (b * CHUNKS + c) * T + 2 * T)
                    for kt in range(KT):
                        act.wait_ge(s_add, (b * CHUNKS + c) * KT + kt + 1)
                        nc.scalar.activation(ybn[c % 2][:, kt], ps_y[c % 2][kt][:], ACT.Identity,
                                             bias=keep["bn_bias"][:, kt:kt + 1],
                                             scale=keep["bn_scale"][:, kt:kt + 1]).then_inc(s_bn, 1)

                def vk_hi(b):
                    act.wait_ge(s_p3, b + 1)
                    nc.scalar.activation(vkh[:].rearrange("p t n -> p (t n)"), ps_p[:],
                                         ACT.Copy).then_inc(s_p4, 1)

                def mt_hi(b, par, bank):
                    act.wait_ge(s_p6, b * 2 + bank + 1)
                    nc.scalar.activation(mth[par][:, 2 * bank:2 * bank + 2, :].rearrange("p t n -> p (t n)"),
                                         ps_p[:], ACT.Copy).then_inc(s_p7, 1)

                def body(b, last, par):
                    for J in range(PAIRS):
                        ahead = J + 1 < PAIRS or not last
                        more = 2 * J + RING < CHUNKS or not last
                        for t in range(T):
                            norm_hi(b, 2 * J, t)
                        if ahead:
                            den_eps(b, J + 1)
                        for t in range(T):
                            norm_hi(b, 2 * J + 1, t)
                            if more:
                                q_hi(b, 2 * J + RING, t)
                        bn(b, 2 * J)
                        if more:
                            for t in range(T - 1):
                                q_hi(b, 2 * J + RING + 1, t)
                        if ahead:
                            rec_hi(b, J + 1)
                        if more:
                            q_hi(b, 2 * J + RING + 1, T - 1)
                        if not last:
                            if J == 1:
                                vk_hi(b + 1)
                            if J >= 2:
                                mt_hi(b + 1, 1 - par, J - 2)
                        bn(b, 2 * J + 1)

                act.sem_inc(s_bn, 2 * KT)
                vk_hi(0)
                for t in range(T):
                    q_hi(0, 0, t)
                for bank in range(2):
                    mt_hi(0, 0, bank)
                    for t in range(2 * bank, 2 * bank + 2):
                        q_hi(0, 1, t)
                den_eps(0, 0)
                for c in range(2, RING):
                    for t in range(T):
                        q_hi(0, c, t)
                rec_hi(0, 0)
                by_batch(act, body)

            @block.vector
            def _(dve):
                def norms(b, c):
                    n = (b * CHUNKS + c) * T

                    def product(t):
                        dve.wait_ge(s_r, n + t + 2)
                        nc.vector.tensor_tensor(qn[t][:], qraw[c % RING][:, t], ps_r[t % 2][:],
                                                ALU.mult).then_inc(s_n, 1)

                    def low(t):
                        dve.wait_ge(s_nh, n + t + 1)
                        nc.vector.tensor_tensor(nl[:, t], qn[t][:], nh[:, t].bitcast(F32),
                                                ALU.subtract).then_inc(s_nl, 1)

                    product(0)
                    for t in range(1, T):
                        product(t)
                        low(t - 1)
                    low(T - 1)

                def invert(b, J):
                    dve.wait_ge(s_de, b * PAIRS + J + 1)
                    nc.vector.reciprocal(den[:], den[:]).then_inc(s_rc, 1)
                    for k in range(2):
                        at, other = slice(k * NH2, (k + 1) * NH2), slice((1 - k) * NH2, (2 - k) * NH2)
                        dve.wait_ge(s_rh, (b * PAIRS + J) * 2 + k + 1)
                        nc.vector.tensor_tensor(rec[k][other, :], den[at, :], rec[k][at, :].bitcast(F32),
                                                ALU.subtract).then_inc(s_rl, 1)

                def prep_diag(b):
                    dve.wait_ge(s_p1, b + 1)
                    sums = ps_p[:, 0:KT * HT * (DIM + 1)].rearrange("p (t h e) -> p t h e", t=KT, h=HT)
                    for t in range(T):
                        if t < KT:
                            vk = keep["vk_a"][:, bass.ds(b, 1), t, 0:DIM].broadcast_to([P, HT, DIM])
                        else:
                            vk = sums[:, t - KT, :, 0:DIM]
                        last = nc.vector.tensor_tensor(vkd[:, t].rearrange("p (h e) -> p h e", e=DIM), vk,
                                                       heads_mask(DIM), ALU.mult)
                    last.then_inc(s_p2, 1)
                    for t in range(T):
                        if t < KT:
                            ks = keep["vk_a"][:, bass.ds(b, 1), t, DIM:].rearrange("p a e -> p (a e)"
                                                                                ).broadcast_to([P, HT])
                        else:
                            ks = sums[:, t - KT, :, DIM]
                        last = nc.vector.tensor_tensor(sd[:, t], ks, keep["headmask"][:], ALU.mult)
                    last.then_inc(s_sf, 1)

                def prep_sden(b):
                    dve.wait_ge(s_sf, b + 1)
                    for t in range(T):
                        at = slice(NH2 + HT * t, NH2 + HT * (t + 1))
                        last = nc.vector.tensor_copy(sdh[:, t, at], sd[:, t])
                    last.then_inc(s_sh, 1)
                    dve.wait_ge(s_sh, b + 1)
                    for t in range(T):
                        at = slice(NH2 + HT * t, NH2 + HT * (t + 1))
                        last = nc.vector.tensor_tensor(sdl[:, t, at], sd[:, t],
                                                       sdh[:, t, at].bitcast(F32), ALU.subtract)
                    last.then_inc(s_sl, 1)

                def vk_lo(b):
                    dve.wait_ge(s_p4, b + 1)
                    nc.vector.tensor_tensor(vkl[:].rearrange("p t n -> p (t n)"), ps_p[:],
                                            vkh[:].rearrange("p t n -> p (t n)").bitcast(F32),
                                            ALU.subtract).then_inc(s_p5, 1)

                def mt_lo(b, par, bank):
                    dve.wait_ge(s_p7, b * 2 + bank + 1)
                    hi, lo = (v[par][:, 2 * bank:2 * bank + 2, :].rearrange("p t n -> p (t n)")
                              for v in (mth, mtl))
                    nc.vector.tensor_tensor(lo, ps_p[:], hi.bitcast(F32), ALU.subtract).then_inc(s_p8, 1)

                def body(b, last, par):
                    for J in range(PAIRS):
                        norms(b, 2 * J)
                        norms(b, 2 * J + 1)
                        if J == PAIRS - 2 and not last:
                            dve.wait_ge(s_de, b * PAIRS + J + 2)
                            prep_sden(b + 1)
                        if J + 1 < PAIRS or not last:
                            invert(b, J + 1)
                        if not last:
                            if J == 0:
                                prep_diag(b + 1)
                            if J == 1:
                                vk_lo(b + 1)
                            if J >= 2:
                                mt_lo(b + 1, 1 - par, J - 2)

                dve.sem_inc(s_rl, 1)
                dve.sem_inc(s_n, 2)
                nc.vector.memset(qn[0][:], 0.0).then_inc(s_z, 1)
                dve.wait_ge(s_z, 1)
                zeros = qn[0][:, 0:3 * NH2].rearrange("p (t n) -> p t n", t=1).broadcast_to([P, T, 3 * NH2])
                for v in (sdh, sdl):
                    nc.vector.tensor_copy(v[:], zeros).then_inc(s_z, 1)
                prep_diag(0)
                dve.wait_ge(s_z, 3)
                prep_sden(0)
                vk_lo(0)
                for bank in range(2):
                    mt_lo(0, 0, bank)
                dve.wait_ge(s_c, 3)
                nc.vector.tensor_copy(spread[:].rearrange("p t n -> p (t n)"),
                                      spread_f[:].rearrange("p t n -> p (t n)")).then_inc(s_z, 1)
                invert(0, 0)
                by_batch(dve, body)

            @block.tensor
            def _(pe):
                def den_tile(b, J, k, t):
                    pe.wait_ge(s_ql, (b * CHUNKS + 2 * J + k) * T + t + 1)
                    cols = slice(NH2, 3 * NH2) if k == 0 else slice(0, 2 * NH2)
                    ws = (sdh[:, t, cols], sdl[:, t, cols])
                    for i, (w, mv) in enumerate(split_passes(ws[0], ws[1], qh[k][:, t], ql[k][:, t])):
                        last = nc.tensor.matmul(ps_den[:], w, mv, start=(t == 0 and k == 0 and i == 0),
                                                stop=(t == T - 1 and k == 1 and i == 2))
                    if k == 1 and t == T - 1:
                        last.then_inc(s_den, 1)

                def den_start(b, J):
                    if J == 0:
                        pe.wait_ge(s_sl, b + 1)

                def spread_rec(b, c, t):
                    if t == 0:
                        pe.wait_ge(s_rl, b * CHUNKS + c + 2)
                    pe.wait_ge(s_n, (b * CHUNKS + c) * T + t + 1)
                    nc.tensor.matmul(ps_r[t % 2][:], spread[:, t], rec[c % 2][:], start=True,
                                     stop=True).then_inc(s_r, 1)

                def project(b, c, par, before):
                    if c == 0:
                        pe.wait_ge(s_p8, b * 2 + 2)
                    pe.wait_ge(s_bn, (b * CHUNKS + c) * KT + KT)
                    for t in range(T):
                        before(t)
                        pe.wait_ge(s_nl, (b * CHUNKS + c) * T + t + 1)
                        for kt in range(KT):
                            ws = [v[par][:, t, kt * P:(kt + 1) * P] for v in (mth, mtl)]
                            for i, (w, mv) in enumerate(split_passes(ws[0], ws[1], nh[:, t], nl[:, t])):
                                last = nc.tensor.matmul(ps_y[c % 2][kt][:], w, mv, start=(t == 0 and i == 0),
                                                        stop=(t == T - 1 and i == 2))
                        last.then_inc(s_y, 1)

                def prep_sums(b):
                    for t in range(KT):
                        n = HT * (DIM + 1)
                        src = keep["vk_b"][:, bass.ds(b, 1), t * HT:(t + 1) * HT, :]
                        last = nc.tensor.matmul(ps_p[:, t * n:(t + 1) * n], keep["dimsel"][:],
                                                src.rearrange("p a h e -> p (a h e)"), start=True, stop=True)
                    last.then_inc(s_p1, 1)

                def prep_transposes(b):
                    pe.wait_ge(s_p2, b + 1)
                    pe.wait_ge(s_sf, b + 1)
                    for t in range(T):
                        last = nc.tensor.transpose(ps_p[:, t * P:(t + 1) * P], vkd[:, t], keep["ident"][:])
                    last.then_inc(s_p3, 1)

                def prep_products(b, bank):
                    if bank == 0:
                        pe.wait_ge(s_p5, b + 1)
                    else:
                        pe.wait_ge(s_p8, b * 2 + 1)
                    for k in range(2):
                        t = 2 * bank + k
                        for i, (w, mv) in enumerate(split_passes(vkh[:, t], vkl[:, t], keep["wp_hi"][:, t],
                                                                 keep["wp_lo"][:, t])):
                            last = nc.tensor.matmul(ps_p[:, k * C:(k + 1) * C], w, mv,
                                                    start=(i == 0), stop=(i == 2))
                    last.then_inc(s_p6, 1)

                def body(b, last, par):
                    for J in range(PAIRS):
                        ahead = J + 1 < PAIRS or not last
                        nb, nJ = (b, J + 1) if J + 1 < PAIRS else (b + 1, 0)
                        if ahead:
                            den_start(nb, nJ)
                            pe.wait_ge(s_de, b * PAIRS + J + 1)
                        for n in range(2 * T):
                            if ahead:
                                den_tile(nb, nJ, n // T, n % T)
                            if n % 2:
                                spread_rec(b, 2 * J, n // 2)
                        project(b, 2 * J, par, lambda t: spread_rec(b, 2 * J + 1, t))
                        if not last:
                            if J == 0:
                                pe.wait_ge(s_p8, b * 2 + 2)
                                prep_sums(b + 1)
                            if J == 1:
                                prep_transposes(b + 1)
                            if J >= 2:
                                prep_products(b + 1, J - 2)
                        project(b, 2 * J + 1, par, lambda t: None)

                pe.sem_inc(s_den, 1)
                pe.sem_inc(s_r, 1)
                pe.sem_inc(s_y, T)
                prep_sums(0)
                prep_transposes(0)
                for bank in range(2):
                    prep_products(0, bank)
                den_start(0, 0)
                for n in range(2 * T):
                    den_tile(0, 0, n // T, n % T)
                pe.wait_ge(s_z, 4)
                by_batch(pe, body)


def bass_conv_linear_attention_kernel(nc, x, w_qkv, w_dw, w_pw, w_proj, bn_gamma, bn_beta, bn_mean, bn_var, out):
    n_batch = x.shape[0]
    grid_d = nc.dram_tensor("grid", [n_batch, PARTS * C, STG], F32, kind="Internal").ap()
    q_d = nc.dram_tensor("relu_q", [n_batch, 2 * C, NPIX], F32, kind="Internal").ap()
    kern_d = nc.dram_tensor("kernels", [PARTS * HEADS, DIM, KROW], F32, kind="Internal").ap()
    x_d = x.rearrange("b c h w -> b c (h w)")
    out_d = out.rearrange("b c h w -> b c (h w)")
    with ExitStack() as ctx:
        keep = kept(nc, ctx, n_batch)
        with ExitStack() as own:
            m = Mem(nc, own)
            keep["xraw"], keep["x_loaded"] = m.sb("xraw", [P, KT, NPIX]), m.sem("x_loaded")
            keep["wq_hi"] = m.sb("wq_hi", [P, KT, PARTS * C], F32R)
            keep["wq_lo"] = m.sb("wq_lo", [P, KT, PARTS * C], F32R)
            phase0_weights(nc, keep, x_d, w_qkv, w_dw, w_pw, w_proj, bn_gamma, bn_beta, bn_mean, bn_var, kern_d)
            phase1_qkv(nc, keep, x_d, grid_d, q_d, n_batch)
        keep["vk_b"] = Mem(nc, ctx).sb("vk_b", [P, n_batch, HEADS, DIM + 1])
        phase2_agg(nc, keep, kern_d, grid_d, q_d, n_batch, HEADS)
        phase3_out(nc, keep, x_d, q_d, out_d, n_batch)


_INS = ["x", "L0_conv_w_qkv", "L0_conv_w_dw", "L0_conv_w_pw", "L0_conv_w_proj", "L0_conv_bn_gamma",
        "L0_conv_bn_beta", "L0_conv_bn_mean", "L0_conv_bn_var"]


def kernel(**inputs):
    import numpy as _np
    import concourse.bacc as _bacc
    from concourse import mybir as _mybir
    from concourse.bass_utils import run_bass_kernel_spmd as _run

    nc = _bacc.Bacc("TRN2", target_bir_lowering=False, num_devices=1)
    arrays, args = {}, []
    for name in _INS:
        a = _np.ascontiguousarray(inputs[name])
        arrays[f"in_{name}"] = a
        args.append(nc.dram_tensor(f"in_{name}", a.shape, _mybir.dt.from_np(a.dtype), kind="ExternalInput").ap())
    args.append(nc.dram_tensor("out_0", inputs["x"].shape, _mybir.dt.float32, kind="ExternalOutput").ap())
    bass_conv_linear_attention_kernel(nc, *args)
    r = _run(nc, [arrays], core_ids=[0])
    return r.results[0]["out_0"]
```
